# Optimizing a Trainium2 kernel written in Bass

```python
import numpy as np
import jax
import jax.numpy as jnp

def _softmax(x, axis=-1):
    return jax.nn.softmax(x, axis=axis)

def _gelu(x):
    return jax.nn.gelu(x, approximate=True)

def _silu(x):
    return jax.nn.silu(x)

def _sigmoid(x):
    return jax.nn.sigmoid(x)

def _layernorm(x, axis=-1, eps=1e-05):
    m = jnp.mean(x, axis=axis, keepdims=True)
    v = jnp.var(x, axis=axis, keepdims=True)
    return (x - m) / jnp.sqrt(v + eps)

def _scatter_add(tgt, idx, src, axis=0):
    return tgt.at[idx].add(src)

def _segment_sum(src, seg, n):
    return jax.ops.segment_sum(src, seg, n)
kernel_name = 'mk_decoder_preln_d1_seqx_r8_40576d'

def setup_inputs(seed: int=0):
    np.random.seed(seed)
    _w = jnp.asarray

    def _rec_inputs():
        import jax
        import jax.numpy as jnp
        _rk = jax.random.key(seed)
        x = -0.000125 + 0.9999 * jax.random.normal(jax.random.fold_in(_rk, 1), (2, 256, 512), jnp.float32)
        _lenS = 256 - jax.random.randint(jax.random.fold_in(_rk, 7), (2,), 0, max(1, 256 // 4) + 1, jnp.int32)
        _lenS2 = 512 - jax.random.randint(jax.random.fold_in(_rk, 8), (2,), 0, max(1, 512 // 4) + 1, jnp.int32)
        _ctx_4096P = jax.random.normal(jax.random.fold_in(_rk, 11), (2, 16, 512), jnp.float32)
        _ctx_4096c = jax.random.dirichlet(jax.random.fold_in(_rk, 511), 0.3 * jnp.ones((16,), jnp.float32), (2, 512))
        _ctx_4096t = jnp.einsum('bsk,bkd->bsd', _ctx_4096c, _ctx_4096P)
        _ctx_4096t = _ctx_4096t * jax.lax.rsqrt(jnp.mean(jnp.square(_ctx_4096t)) + 1e-12) * 0.953939
        ctx_4096 = -5.72187e-05 + 0.999849 * (_ctx_4096t + 0.3 * jax.random.normal(jax.random.fold_in(_rk, 611), (2, 512, 512), jnp.float32))
        return (x, ctx_4096)
    x, ctx_4096 = _rec_inputs()

    def _L0_attn_setup():
        import jax, jax.numpy as jnp
        import numpy as np
        Q_DIM = 512
        N_HEADS = 32
        HEAD_DIM = 128
        INNER = N_HEADS * HEAD_DIM
        EPS = 1e-06

        def rms_norm(x, w):
            xf = x.astype(jnp.float32)
            var = jnp.mean(xf * xf, axis=-1, keepdims=True)
            return (w.astype(jnp.float32) * xf * jax.lax.rsqrt(var + EPS)).astype(x.dtype)
        key = jax.random.key(seed)
        ks = jax.random.split(key, 12)
        s = 1.0 / np.sqrt(Q_DIM)
        return {'hidden_states': jax.random.normal(ks[0], (2, 256, Q_DIM), dtype=jnp.float32), 'Wq': jax.random.normal(ks[1], (Q_DIM, INNER), dtype=jnp.float32) * s, 'bq': jnp.zeros((INNER,), dtype=jnp.float32), 'Wk': jax.random.normal(ks[2], (Q_DIM, INNER), dtype=jnp.float32) * s, 'bk': jnp.zeros((INNER,), dtype=jnp.float32), 'Wv': jax.random.normal(ks[3], (Q_DIM, INNER), dtype=jnp.float32) * s, 'bv': jnp.zeros((INNER,), dtype=jnp.float32), 'Wo': jax.random.normal(ks[4], (INNER, Q_DIM), dtype=jnp.float32) * s, 'bo': jnp.zeros((Q_DIM,), dtype=jnp.float32), 'gq': jnp.ones((INNER,), dtype=jnp.float32), 'gk': jnp.ones((INNER,), dtype=jnp.float32)}
    _L0_attn_all = _L0_attn_setup()
    _L0_attn_in = {k: v for k, v in _L0_attn_all.items() if k in ('Wq', 'bq', 'Wk', 'bk', 'Wv', 'bv', 'Wo', 'bo', 'gq', 'gk')}
    del _L0_attn_all

    def _L0_xattn_setup():
        import jax, jax.numpy as jnp
        import numpy as np
        QMIN = 0.0
        QMAX = 255.0

        def fake_quant(x, scale, zp):
            s = scale.reshape(())
            z = zp.reshape(())
            q = jnp.clip(jnp.round(x / s + z), QMIN, QMAX)
            return (q - z) * s
        key = jax.random.key(seed)
        k1, k2 = jax.random.split(key)
        B, M, K, N = (4, 256, 512, 512)
        x1 = jax.random.normal(k1, (B, M, K), dtype=jnp.float32)
        x2 = jax.random.normal(k2, (B, K, N), dtype=jnp.float32)
        x1_scale = jnp.full((1,), 8.0 / 255.0, dtype=jnp.float32)
        x1_zp = jnp.full((1,), 128.0, dtype=jnp.float32)
        x2_scale = jnp.full((1,), 8.0 / 255.0, dtype=jnp.float32)
        x2_zp = jnp.full((1,), 128.0, dtype=jnp.float32)
        return {'x1': x1, 'x2': x2, 'x1_scale': x1_scale, 'x1_zp': x1_zp, 'x2_scale': x2_scale, 'x2_zp': x2_zp}
    _L0_xattn_all = _L0_xattn_setup()
    _L0_xattn_in = {k: v for k, v in _L0_xattn_all.items() if k in ('x1_scale', 'x1_zp', 'x2_scale', 'x2_zp')}
    del _L0_xattn_all

    def _L0_ffn_setup():
        import jax, jax.numpy as jnp
        import numpy as np
        SCALING = 32.0 / 16.0
        key = jax.random.key(seed)
        ks = jax.random.split(key, 7)
        B, T, D, O, R, E = (4, 256, 512, 512, 16, 8)
        x = jax.random.normal(ks[0], (B, T, D), dtype=jnp.float32)
        base_W = jax.random.normal(ks[1], (O, D), dtype=jnp.float32) * D ** (-0.5)
        base_b = jax.random.normal(ks[2], (O,), dtype=jnp.float32) * 0.01
        router_W = jax.random.normal(ks[3], (2 * E - 1, D), dtype=jnp.float32) * D ** (-0.5)
        router_b = jax.random.normal(ks[4], (2 * E - 1,), dtype=jnp.float32) * 0.01
        A = jax.random.normal(ks[5], (E, R, D), dtype=jnp.float32) * D ** (-0.5)
        Bm = jax.random.normal(ks[6], (E, O, R), dtype=jnp.float32) * R ** (-0.5)
        assigned_idx = 0
        others = [i for i in range(E) if i != assigned_idx]
        expert_map = jnp.array([assigned_idx] * E + others, dtype=jnp.int32)
        return {'x': x, 'base_W': base_W, 'base_b': base_b, 'router_W': router_W, 'router_b': router_b, 'A': A, 'B': Bm, 'expert_map': expert_map}
    _L0_ffn_all = _L0_ffn_setup()
    _L0_ffn_in = {k: v for k, v in _L0_ffn_all.items() if k in ('base_W', 'base_b', 'router_W', 'router_b', 'A', 'B', 'expert_map')}
    del _L0_ffn_all
    return {'x': x, 'ctx_4096': ctx_4096, 'L0_attn_Wq': _L0_attn_in['Wq'], 'L0_attn_bq': _L0_attn_in['bq'], 'L0_attn_Wk': _L0_attn_in['Wk'], 'L0_attn_bk': _L0_attn_in['bk'], 'L0_attn_Wv': _L0_attn_in['Wv'], 'L0_attn_bv': _L0_attn_in['bv'], 'L0_attn_Wo': _L0_attn_in['Wo'], 'L0_attn_bo': _L0_attn_in['bo'], 'L0_attn_gq': _L0_attn_in['gq'], 'L0_attn_gk': _L0_attn_in['gk'], 'L0_xattn_x1_scale': _L0_xattn_in['x1_scale'], 'L0_xattn_x1_zp': _L0_xattn_in['x1_zp'], 'L0_xattn_x2_scale': _L0_xattn_in['x2_scale'], 'L0_xattn_x2_zp': _L0_xattn_in['x2_zp'], 'L0_ffn_base_W': _L0_ffn_in['base_W'], 'L0_ffn_base_b': _L0_ffn_in['base_b'], 'L0_ffn_router_W': _L0_ffn_in['router_W'], 'L0_ffn_router_b': _L0_ffn_in['router_b'], 'L0_ffn_A': _L0_ffn_in['A'], 'L0_ffn_B': _L0_ffn_in['B'], 'L0_ffn_expert_map': _L0_ffn_in['expert_map']}

def reference(x, ctx_4096, L0_attn_Wq, L0_attn_bq, L0_attn_Wk, L0_attn_bk, L0_attn_Wv, L0_attn_bv, L0_attn_Wo, L0_attn_bo, L0_attn_gq, L0_attn_gk, L0_xattn_x1_scale, L0_xattn_x1_zp, L0_xattn_x2_scale, L0_xattn_x2_zp, L0_ffn_base_W, L0_ffn_base_b, L0_ffn_router_W, L0_ffn_router_b, L0_ffn_A, L0_ffn_B, L0_ffn_expert_map):
    import jax
    import jax.numpy as jnp

    def _L0_attn_ref(hidden_states, Wq, bq, Wk, bk, Wv, bv, Wo, bo, gq, gk):
        import jax, jax.numpy as jnp
        import numpy as np
        Q_DIM = 512
        N_HEADS = 32
        HEAD_DIM = 128
        INNER = N_HEADS * HEAD_DIM
        EPS = 1e-06

        def rms_norm(x, w):
            xf = x.astype(jnp.float32)
            var = jnp.mean(xf * xf, axis=-1, keepdims=True)
            return (w.astype(jnp.float32) * xf * jax.lax.rsqrt(var + EPS)).astype(x.dtype)
        B, S, _ = hidden_states.shape
        q = hidden_states @ Wq + bq
        k = hidden_states @ Wk + bk
        v = hidden_states @ Wv + bv
        q = rms_norm(q, gq)
        k = rms_norm(k, gk)
        q = q.reshape(B, S, N_HEADS, HEAD_DIM).transpose(0, 2, 1, 3)
        k = k.reshape(B, S, N_HEADS, HEAD_DIM).transpose(0, 2, 1, 3)
        v = v.reshape(B, S, N_HEADS, HEAD_DIM).transpose(0, 2, 1, 3)
        scale = 1.0 / np.sqrt(HEAD_DIM)
        attn = jnp.einsum('bhqd,bhkd->bhqk', q.astype(jnp.float32), k.astype(jnp.float32)) * scale
        attn = jax.nn.softmax(attn, axis=-1)
        out = jnp.einsum('bhqk,bhkd->bhqd', attn, v.astype(jnp.float32))
        out = out.transpose(0, 2, 1, 3).reshape(B, S, INNER).astype(hidden_states.dtype)
        return out @ Wo + bo

    def _L0_xattn_ref(x1, x2, x1_scale, x1_zp, x2_scale, x2_zp):
        import jax, jax.numpy as jnp
        import numpy as np
        QMIN = 0.0
        QMAX = 255.0

        def fake_quant(x, scale, zp):
            s = scale.reshape(())
            z = zp.reshape(())
            q = jnp.clip(jnp.round(x / s + z), QMIN, QMAX)
            return (q - z) * s
        q1 = fake_quant(x1, x1_scale, x1_zp)
        q2 = fake_quant(x2, x2_scale, x2_zp)
        return jnp.matmul(q1, q2)

    def _L0_ffn_ref(x, base_W, base_b, router_W, router_b, A, B, expert_map):
        import jax, jax.numpy as jnp
        import numpy as np
        SCALING = 32.0 / 16.0
        E = A.shape[0]
        base_out = jnp.einsum('btd,od->bto', x, base_W) + base_b
        logits = jnp.einsum('btd,nd->btn', x, router_W) + router_b
        probs = jax.nn.softmax(logits, axis=-1)
        topk_p, topk_i = jax.lax.top_k(probs, E)
        mapped = expert_map[topk_i]
        onehot = (mapped[..., None] == jnp.arange(E)).astype(x.dtype)
        w = jnp.einsum('btk,btke->bte', topk_p, onehot)
        h = jnp.einsum('btd,erd->bter', x, A)
        lora = jnp.einsum('bter,eor->bto', h * w[..., None], B) * SCALING
        return base_out + lora
    x = x + _L0_attn_ref(_layernorm(x, axis=-1), L0_attn_Wq, L0_attn_bq, L0_attn_Wk, L0_attn_bk, L0_attn_Wv, L0_attn_bv, L0_attn_Wo, L0_attn_bo, L0_attn_gq, L0_attn_gk)
    x = x + _L0_xattn_ref(_layernorm(x, axis=-1), ctx_4096, L0_xattn_x1_scale, L0_xattn_x1_zp, L0_xattn_x2_scale, L0_xattn_x2_zp)
    x = x + _L0_ffn_ref(_layernorm(x, axis=-1), L0_ffn_base_W, L0_ffn_base_b, L0_ffn_router_W, L0_ffn_router_b, L0_ffn_A, L0_ffn_B, L0_ffn_expert_map)
    return x

_drawn_inputs = setup_inputs


def setup_inputs(seed=0):
    import zlib

    import numpy as np

    out = dict(_drawn_inputs(seed))
    spreads = {'L0_attn_bq': (0.0, 0.318),
     'L0_attn_bk': (0.0, 0.8),
     'L0_attn_bv': (0.0, 0.1),
     'L0_attn_bo': (0.0, 0.1),
     'L0_attn_gq': (1.0, 0.2),
     'L0_attn_gk': (1.0, 0.2)}
    factors = {'L0_ffn_base_b': 64.0, 'L0_ffn_router_b': 191.64}
    for name, (base, spread) in spreads.items():
        noise = np.random.default_rng([zlib.crc32(name.encode()), seed]).standard_normal(out[name].shape)
        drawn = base * np.exp(spread * noise) if base else spread * noise
        out[name] = jnp.asarray(drawn.astype(out[name].dtype))
    for name, factor in factors.items():
        out[name] = (out[name] * factor).astype(out[name].dtype)
    return out
```

```python
from contextlib import ExitStack

import concourse.bass as bass
from concourse import mybir

F32 = mybir.dt.float32
F32R = mybir.dt.float32r
BF16 = mybir.dt.bfloat16
I32 = mybir.dt.int32
ALU = mybir.AluOpType
ACT = mybir.ActivationFunctionType
AX = mybir.AxisListType

P = 128
B, S, D = 2, 256, 512
T = B * S
NT = T // P
NC = D // P
SKV = 512
NH, DH = 32, 128
NP = NH // 2
NS = 2 * NH
PW = 2 * DH
INNER = NH * DH
NE, RK, NR = 8, 16, 15
RA = P + NR + 1
EPS_LN, EPS_RMS = 1e-5, 1e-6
ROUND = 12582912.0
MID = 128.0
QMIN, QMAX = 0.0, 255.0
U1 = 2 * NH


def decoder_layer(nc, x, ctx_t, wk, wq, wv, wo, bk, bq, bv, bo, gk, gq, qscal, ra_w, base_b, router_b, bm_w,
                  expert_map, out):
    st = ExitStack()
    with st:
        def sem(name):
            return st.enter_context(nc.semaphore(name))

        def bank(name, shape, dt=F32):
            return st.enter_context(nc.psum_tensor(name, shape, dt))

        base = (nc.sbuf_base + 63) // 64 * 64
        top = [base]

        def place(name, shape, dt, at=None):
            size = {F32: 4, F32R: 4, BF16: 2, I32: 4}[dt]
            for n in shape[1:]:
                size *= n
            if at is None:
                at = top[0]
                top[0] += (size + 31) // 32 * 32
            return nc.alloc_sbuf_tensor_at(name, shape, dt, offset=at), at

        def here(name, shape, dt, at=None):
            return place(name, shape, dt, at)[0]

        xnt_hi = here("xnt_hi", [P, NC, T], F32R)
        xnt_lo = here("xnt_lo", [P, NC, T], F32R)
        k_all, k_at = place("k_all", [P, NH, T], F32)
        q_all, q_at = place("q_all", [P, NH, T], F32)
        v_hi, vh_at = place("v_hi", [P, 2, NT, PW], F32R)
        v_lo, vl_at = place("v_lo", [P, 2, NT, PW], F32R)
        k_hi, kh_at = place("k_hi", [P, T], F32R)
        k_lo, kl_at = place("k_lo", [P, T], F32R)
        q_hi, qh_at = place("q_hi", [P, T], F32R)
        q_lo, ql_at = place("q_lo", [P, T], F32R)
        pt_hi, pt_at = place("pt_hi", [P, 2, S], F32R)
        pt_lo = here("pt_lo", [P, 2, S], F32R)
        o_hi = here("o_hi", [P, T], F32R)
        o_lo = here("o_lo", [P, T], F32R)
        wo_hi = here("wo_hi", [P, D], F32R)
        wo_lo = here("wo_lo", [P, D], F32R)
        raw, raw_at = place("raw", [P, 4, 512], F32)
        probs = here("probs", [P, 2, 2, S], F32, raw_at + 2 * 2048)
        w_hi = here("w_hi", [P, 2, NC * PW], F32R)
        w_lo = here("w_lo", [P, 2, NC * PW], F32R)
        ident = here("ident", [P, P], F32)
        ident_b = here("ident_b", [P, P], BF16)
        ones = here("ones", [P, P], F32)
        bk_c = here("bk_c", [P, NH], F32)
        bq_c = here("bq_c", [P, NH], F32)
        bv_c = here("bv_c", [P, NH], F32)
        g_c = here("g_c", [P, NH], F32)
        gq_c = here("gq_c", [P, NH], F32)
        mhalf = here("mhalf", [P, NT], F32)
        ssq = here("ssq", [P, NT], F32)
        rk_t = here("rk_t", [P, NT], F32)
        rq_t = here("rq_t", [P, NT], F32)
        nmax = here("nmax", [P, 2, 2], F32)
        nbias = here("nbias", [P, 2, 2], F32)
        rsum = here("rsum", [P, 2, 2], F32)
        rinv = here("rinv", [P, 2, 2], F32)
        stats = here("stats", [P, NT, 6], F32)
        mv = here("mv", [P, NT, 2], F32)
        vare = here("vare", [P, NT], F32)
        rstd = here("rstd", [P, NT], F32)
        sc = here("sc", [P, 8], F32)
        assert top[0] <= nc.sbuf_usable_end, (top[0], nc.sbuf_usable_end)

        half = NT * PW * 4
        acc_k = here("acc_k", [P, T], F32, vh_at + half)
        acc_q = here("acc_q", [P, T], F32, vh_at + half + 2048)
        rkb = here("rkb", [P, T], F32, vl_at + half)
        diag = here("diag", [P, NT, P], F32, vl_at + half + 2048)
        square = here("square", [P, 2, T], F32, pt_at)
        xin = here("xin", [P, NT, D], F32, q_at + (NH - NT) * T * 4)
        KS = T * 4
        x_res = here("x_res", [P, NT, D], F32, k_at)
        ctx_f = here("ctx_f", [P, B * NC, SKV], F32, k_at + 4 * KS)
        ctx_q = here("ctx_q", [P, B * NC, SKV], BF16, k_at + 12 * KS)
        ra_f = here("ra_f", [P, NC * RA], F32, k_at + 16 * KS)
        bm_f = here("bm_f", [P, D], F32, k_at + 18 * KS)
        bo_b = here("bo_b", [P, D], F32, k_at + 19 * KS)
        bb_b = here("bb_b", [P, D], F32, k_at + 20 * KS)
        rb_b = here("rb_b", [P, NR], F32, k_at + 21 * KS)
        em_i = here("em_i", [P, NR], I32, k_at + 21 * KS + 64)
        qs_b = here("qs_b", [P, 4], F32, k_at + 21 * KS + 128)
        xn = here("xn", [P, NT, D], F32, q_at)
        q1 = here("q1", [P, NT, D], BF16, q_at + 4 * KS)
        q1t = here("q1t", [P, NT, NC, P], BF16, q_at + 6 * KS)
        corr = here("corr", [P, B, SKV], F32, q_at + 8 * KS)
        hw = here("hw", [P, NT, P], F32, q_at + 10 * KS)
        ones_b = here("ones_b", [P, P], BF16, q_at + 11 * KS)
        small_at = q_at + 12 * KS
        emf = here("emf", [P, NR], F32, small_at)
        onehot = here("onehot", [P, NE, NR], F32, small_at + 128)
        logit = here("logit", [P, NT, NR], F32, small_at + 1024)
        pr = here("pr", [P, NT, NR], F32, small_at + 1536)
        top8 = here("top8", [P, NT, 8], F32, small_at + 2048)
        cut = here("cut", [P, NT, NR], F32, small_at + 2304)
        kept = here("kept", [P, NT, NR], F32, small_at + 2560)
        spread = here("spread", [P, NT, NE, NR], F32, small_at + 3072)
        gate = here("gate", [P, NT, NE], F32, small_at + 5120)
        fsm = here("fsm", [P, NT, 4], F32, small_at + 5376)
        rsd = here("rsd", [P, NT], F32, small_at + 5632)
        qc = here("qc", [P, 8], F32, small_at + 5760)
        ra_hi = here("ra_hi", [P, NC * RA], F32R, vh_at)
        ra_lo = here("ra_lo", [P, NC * RA], F32R, vl_at)
        bm_hi = here("bm_hi", [P, D], F32R, kh_at)
        bm_lo = here("bm_lo", [P, D], F32R, kl_at)
        hwt_hi = here("hwt_hi", [P, NT, P], F32R, qh_at)
        hwt_lo = here("hwt_lo", [P, NT, P], F32R, ql_at)

        acc = [bank(f"acc{t}", [P, D]) for t in range(NT)]
        p_v = bank("p_v", [P, 2, PW])
        p_s = bank("p_s", [P, 2, S])
        p_t = bank("p_t", [P, 2, S])
        p_o = bank("p_o", [P, T])
        p_rows = [p_v, p_s, p_t, p_o]
        p_flat = [p_v[:].rearrange("p a b -> p (a b)"), p_s[:].rearrange("p a b -> p (a b)"),
                  p_t[:].rearrange("p a b -> p (a b)"), p_o[:]]

        x_landed = [sem(f"x_landed{t}") for t in range(NT)]
        const_landed = sem("const_landed")
        w_landed = [sem(f"w_landed{r}") for r in range(4)]
        consts_made = sem("consts_made")
        gpow = sem("gpow")
        ln_var = sem("ln_var")
        ln_done = sem("ln_done")
        xt_ready = sem("xt_ready")
        xt_hi = sem("xt_hi")
        xt_lo = sem("xt_lo")
        w_hi_done = sem("w_hi_done")
        w_lo_dve = sem("w_lo_dve")
        w_lo_pool = sem("w_lo_pool")
        proj_ready = sem("proj_ready")
        squared = sem("squared")
        summed = sem("summed")
        ssq_ready = sem("ssq_ready")
        ssq_out = sem("ssq_out")
        rms_pow = sem("rms_pow")
        diag_made = sem("diag_made")
        rkb_ready = sem("rkb_ready")
        rkb_out = sem("rkb_out")
        k_normed = sem("k_normed")
        kq_hi = sem("kq_hi")
        kq_lo = sem("kq_lo")
        scores_ready = sem("scores_ready")
        max_done = sem("max_done")
        nb_done = sem("nb_done")
        exp_done = sem("exp_done")
        rinv_done = sem("rinv_done")
        p_normed = sem("p_normed")
        pt_ready = sem("pt_ready")
        pt_hi_done = sem("pt_hi_done")
        pt_lo_done = sem("pt_lo_done")
        pv_done = sem("pv_done")
        o_hi_done = sem("o_hi_done")
        o_lo_done = sem("o_lo_done")
        v_ready = sem("v_ready")
        v_hi_done = sem("v_hi_done")
        v_lo_done = sem("v_lo_done")
        wo_used = sem("wo_used")
        tail_landed = [sem(f"tail_landed{n}") for n in range(8)]
        stored = sem("stored")
        chain = sem("chain")
        t_xres = sem("t_xres")
        t_ctxq = sem("t_ctxq")
        t_ones = sem("t_ones")
        t_col = sem("t_col")
        t_corr = sem("t_corr")
        t_x1 = sem("t_x1")
        t_var = sem("t_var")
        t_pow = sem("t_pow")
        t_lin = sem("t_lin")
        t_xn = sem("t_xn")
        t_q1 = sem("t_q1")
        t_q1t = sem("t_q1t")
        t_q1t_out = sem("t_q1t_out")
        t_qq = sem("t_qq")
        t_x2 = sem("t_x2")
        t_hi = sem("t_hi")
        t_lo = sem("t_lo")
        t_x3t = sem("t_x3t")
        t_x3hi = sem("t_x3hi")
        t_x3lo = sem("t_x3lo")
        t_ra = sem("t_ra")
        t_nmax = sem("t_nmax")
        t_exp = sem("t_exp")
        t_hw = sem("t_hw")
        t_hwt = sem("t_hwt")
        t_hwhi = sem("t_hwhi")
        t_hwlo = sem("t_hwlo")
        t_y = sem("t_y")
        t_out = sem("t_out")

        def head(a, h):
            return a[:, bass.ds(h, 1), :].rearrange("p a t -> p (a t)")

        def column(a, h):
            return a[:, bass.ds(h, 1)]

        def parts(n):
            return [w[:, n, 0:NC * DH].rearrange("p (c n) -> p c n", c=NC) for w in (w_hi, w_lo)]

        def pair_parts(n):
            return [w[:, n, :].rearrange("p (c n) -> p c n", c=NC) for w in (w_hi, w_lo)]


        block = st.enter_context(nc.Block())

        @block.sync
        def _(sp):
            for t in range(NT):
                sp.dma_start(xin[:, t, :], x[t]).then_inc(x_landed[t], 16)
            for r in range(4):
                sp.dma_start(raw[:, r, :], wk[r]).then_inc(w_landed[r], 16)
            for dst, src in ((bk_c, bk), (bq_c, bq), (bv_c, bv), (g_c, gk), (gq_c, gq)):
                sp.dma_start(dst[:], src).then_inc(const_landed, 16)

            def load_heads(w, i, before):
                for r in range(4):
                    sp.wait_ge(w_lo_dve, before + 4 * i + r - 3)
                    sp.dma_start(raw[:, r, :], w[bass.ds(4 * i + r, 1)].rearrange("a p n -> (a p) n")
                                 ).then_inc(w_landed[r], 16)

            with sp.Fori(1, NH // 4) as i:
                load_heads(wk, i, 0)
            with sp.Fori(0, NH // 4) as i:
                load_heads(wq, i, NH)

            def load_wv(pair, c, n):
                sp.dma_start(raw[:, n, :], wv[bass.ds(2 * pair + c, 1)].rearrange("a p n -> (a p) n")
                             ).then_inc(w_landed[n], 16)

            def load_wo(h):
                sp.dma_start(raw[:, 1, :], wo[bass.ds(h, 1)].rearrange("a p n -> (a p) n")
                             ).then_inc(w_landed[1], 16)

            for n in range(4):
                sp.wait_ge(w_lo_dve, U1 - 3 + n if n < 2 else U1 + n - 1)
                load_wv(n // 2, n % 2, n % 2)

            def pair_loads(p):
                for j in range(4):
                    if isinstance(p, int) and j < 2:
                        sp.wait_ge(w_lo_dve, U1 + 3 + j)
                    else:
                        sp.wait_ge(w_lo_pool, 4 * p + j - 1)
                    if j % 2:
                        load_wo(2 * p + j // 2)
                    else:
                        load_wv(p + 2, j // 2, 0)

            pair_loads(0)
            with sp.Fori(1, 12) as p:
                pair_loads(p)
            sp.wait_ge(scores_ready, 2 * 22)
            sp.dma_start(qs_b[:], qscal.partition_broadcast(P)).then_inc(tail_landed[0], 16)
            sp.dma_start(ctx_f[:], ctx_t).then_inc(tail_landed[1], 16)
            sp.dma_start(ra_f[:], ra_w).then_inc(tail_landed[2], 16)
            sp.dma_start(bo_b[:], bo.partition_broadcast(P)).then_inc(tail_landed[3], 16)
            for t in range(NT):
                sp.dma_start(x_res[:, t, :], x[t]).then_inc(tail_landed[3], 16)
            sp.dma_start(bm_f[:], bm_w).then_inc(tail_landed[4], 16)
            sp.dma_start(bb_b[:], base_b.partition_broadcast(P)).then_inc(tail_landed[5], 16)
            sp.dma_start(rb_b[:], router_b.partition_broadcast(P)).then_inc(tail_landed[6], 16)
            sp.dma_start(em_i[:], expert_map.partition_broadcast(P)).then_inc(tail_landed[7], 16)
            with sp.Fori(12, NP) as p:
                pair_loads(p)
            for t in range(NT):
                sp.wait_ge(t_out, t + 1)
                sp.dma_start(out[t], xn[:, t, :]).then_inc(stored, 16)
            sp.wait_ge(stored, 16 * NT)

        def quant_product(pe, t):
            b = t // 2
            pe.wait_ge(t_q1t_out, t + 1)
            pe.wait_ge(t_x1, t + 1)
            if t == 0:
                pe.wait_ge(t_corr, 2)
            for c in range(NC):
                pe.matmul(acc[t][:], q1t[:, t, c, :], ctx_q[:, b * NC + c, :], start=(c == 0), stop=(c == NC - 1))
            if t >= 2:
                pe.wait_ge(t_x2, t - 1)
            for c in range(NC):
                mm = pe.matmul(p_flat[t % 2][:, 0:1], q1t[:, t, c, :], ones_b[:, 0:1],
                               start=(c == 0), stop=(c == NC - 1))
            mm.then_inc(t_qq, 1)

        def low_rank(pe, t):
            pe.wait_ge(t_x3lo, t + 1)
            if t == 0:
                pe.wait_ge(t_lo, 1)
            hi = ra_hi[:].rearrange("p (c n) -> p c n", c=NC)
            lo = ra_lo[:].rearrange("p (c n) -> p c n", c=NC)
            tt = slice(t * P, (t + 1) * P)
            dst = acc[t][:, 0:RA]
            for c in range(NC):
                pe.matmul(dst, xnt_hi[:, c, tt], hi[:, c, :], start=(c == 0), stop=False)
                pe.matmul(dst, xnt_hi[:, c, tt], lo[:, c, :], start=False, stop=False)
                mm = pe.matmul(dst, xnt_lo[:, c, tt], hi[:, c, :], start=False, stop=(c == NC - 1))
            mm.then_inc(t_ra, 1)

        def base_out(pe, t):
            tt = slice(t * P, (t + 1) * P)
            if t == 0:
                pe.wait_ge(w_lo_pool, NS)
                pe.wait_ge(t_x2, NT)
            for g in range(2):
                hi, lo = pair_parts(g)
                dst = p_flat[t][:, g * PW:(g + 1) * PW]
                for c in range(NC):
                    pe.matmul(dst, xnt_hi[:, c, tt], hi[:, c, :], start=(g == 0 and c == 0), stop=False,
                              skip_group_check=True)
                    pe.matmul(dst, xnt_hi[:, c, tt], lo[:, c, :], start=False, stop=False, skip_group_check=True)
                    pe.matmul(dst, xnt_lo[:, c, tt], hi[:, c, :], start=False, stop=False, skip_group_check=True)

        @block.tensor
        def _(pe):
            pe.wait_ge(consts_made, 1)
            for t in range(NT):
                pe.wait_ge(ln_done, t + 1)
                for c in range(NC):
                    mm = pe.transpose(acc[t][:, c * P:(c + 1) * P], xin[:, t, c * P:(c + 1) * P], ident[:])
                mm.then_inc(xt_ready, 1)

            def project(i, r, before):
                u = before + 4 * i + r
                n = r % 2
                pe.wait_ge(w_lo_dve, u + 1)
                if not (isinstance(u, int) and u < 2):
                    pe.wait_ge(squared, u - 1)
                hi, lo = parts(n)
                for c in range(NC):
                    pe.matmul(acc[n][:], hi[:, c, :], xnt_hi[:, c, :], start=(c == 0), stop=False)
                    pe.matmul(acc[n][:], lo[:, c, :], xnt_hi[:, c, :], start=False, stop=False)
                    mm = pe.matmul(acc[n][:], hi[:, c, :], xnt_lo[:, c, :], start=False, stop=(c == NC - 1))
                mm.then_inc(proj_ready, 1)

            def sum_squares(sums, dst, n):
                pe.wait_ge(summed, n)
                for t in range(NT):
                    mm = pe.matmul(dst[:, t:t + 1], sums[:, t * P:(t + 1) * P], ones[:, 0:1],
                                   start=True, stop=True)
                mm.then_inc(ssq_ready, 1)

            pe.wait_ge(xt_lo, NT)
            for r in range(4):
                project(0, r, 0)
            with pe.Fori(1, NH // 4) as i:
                for r in range(4):
                    project(i, r, 0)
            project(0, 0, NH)
            sum_squares(acc_k, p_flat[0], NH)
            project(0, 1, NH)
            pe.wait_ge(diag_made, NT)
            pe.matmul(p_flat[1], ones[:], diag[:].rearrange("p t n -> p (t n)"), start=True, stop=True
                      ).then_inc(rkb_ready, 1)
            project(0, 2, NH)
            project(0, 3, NH)
            with pe.Fori(1, NH // 4) as i:
                for r in range(4):
                    project(i, r, NH)

            def scores(h, b):
                s = 2 * h + b
                if b == 0:
                    pe.wait_ge(kq_lo, 2 * h + 2)
                if not (isinstance(s, int) and s == 0):
                    pe.wait_ge(exp_done, 2 * s)
                kb = slice(b * S, (b + 1) * S)
                for a in range(2):
                    qa = slice(b * S + a * P, b * S + (a + 1) * P)
                    pe.matmul(p_s[:, a, :], q_hi[:, qa], k_hi[:, kb], start=True, stop=False)
                    pe.matmul(p_s[:, a, :], q_lo[:, qa], k_hi[:, kb], start=False, stop=False)
                    mm = pe.matmul(p_s[:, a, :], q_hi[:, qa], k_lo[:, kb], start=False, stop=True)
                mm.then_inc(scores_ready, 1)

            def transpose_probs(s, b):
                pe.wait_ge(p_normed, s + 1)
                for m in range(2):
                    for a in range(2):
                        mm = pe.transpose(p_t[:, m, a * P:(a + 1) * P],
                                          probs[:, b, a, m * P:(m + 1) * P], ident[:])
                mm.then_inc(pt_ready, 1)

            def v_tile(pair, t, par, by, split):
                if t == 0:
                    pe.wait_ge(by, split)
                e = 2 * pair + t // 2
                if t % 2 == 0 and not (isinstance(e, int) and e == 0):
                    pe.wait_ge(v_lo_done, e)
                hi, lo = pair_parts(par)
                tt = slice(t * P, (t + 1) * P)
                for c in range(NC):
                    pe.matmul(p_v[:, t % 2, :], xnt_hi[:, c, tt], hi[:, c, :], start=(c == 0), stop=False)
                    pe.matmul(p_v[:, t % 2, :], xnt_hi[:, c, tt], lo[:, c, :], start=False, stop=False)
                    mm = pe.matmul(p_v[:, t % 2, :], xnt_lo[:, c, tt], hi[:, c, :], start=False,
                                   stop=(c == NC - 1))
                if t % 2:
                    mm.then_inc(v_ready, 1)

            def project_out(h, b, first, last):
                if b == 0:
                    pe.wait_ge(o_lo_done, h + 1)
                    pe.wait_ge(w_lo_pool, 2 * h + 2)
                for t in (2 * b, 2 * b + 1):
                    tt = slice(t * P, (t + 1) * P)
                    pe.matmul(acc[t][:], o_hi[:, tt], wo_hi[:], start=first, stop=False, skip_group_check=True)
                    pe.matmul(acc[t][:], o_lo[:, tt], wo_hi[:], start=False, stop=False, skip_group_check=True)
                    mm = pe.matmul(acc[t][:], o_hi[:, tt], wo_lo[:], start=False, stop=last,
                                   skip_group_check=True)
                if b == 1:
                    mm.then_inc(wo_used, 1)

            def probs_v(h, hin, b, par):
                s = 2 * h + b
                pe.wait_ge(pt_lo_done, s + 1)
                for m in range(2):
                    cols = slice(hin * DH, (hin + 1) * DH)
                    vh, vl = v_hi[:, par, 2 * b + m, cols], v_lo[:, par, 2 * b + m, cols]
                    dst = p_o[:, b * S:(b + 1) * S]
                    pe.matmul(dst, vh, pt_hi[:, m, :], start=(m == 0), stop=False)
                    pe.matmul(dst, vl, pt_hi[:, m, :], start=False, stop=False)
                    mm = pe.matmul(dst, vh, pt_lo[:, m, :], start=False, stop=(m == 1))
                mm.then_inc(pv_done, 1)

            def pair(p, par, first=False, last=False):
                for j in range(4):
                    b = j % 2
                    h = 2 * p + j // 2
                    s = 2 * h + b
                    if not (last and j == 3):
                        scores(h + b, 1 - b)
                    transpose_probs(s, b)
                    if not last:
                        if first:
                            v_tile(p + 1, j, 1 - par, w_lo_dve, U1 + 4)
                        else:
                            v_tile(p + 1, j, 1 - par, w_lo_pool, 4 * p - 1)
                    if not (first and j < 2):
                        project_out(h - 1, b, first=(first and j >= 2), last=False)
                    if j == 0:
                        pe.wait_ge(v_lo_done, 2 * p + 2)
                    probs_v(h, j // 2, b, par)

            v_tile(0, 0, 0, w_lo_dve, U1 + 2)
            v_tile(0, 1, 0, w_lo_dve, U1 + 2)
            scores(0, 0)
            sum_squares(acc_q, p_flat[2], U1)
            v_tile(0, 2, 0, w_lo_dve, U1 + 2)
            v_tile(0, 3, 0, w_lo_dve, U1 + 2)
            pe.wait_ge(ssq_out, 2)
            pair(0, 0, first=True)
            with pe.Fori(0, (NP - 2) // 2) as i:
                pair(2 * i + 1, 1)
                pair(2 * i + 2, 0)
            pair(NP - 1, 1, last=True)
            project_out(NH - 1, 0, False, True)
            project_out(NH - 1, 1, False, True)

            pe.wait_ge(t_ones, 1)
            for b in range(B):
                pe.wait_ge(t_ctxq, 2 * (b + 1))
                for c in range(NC):
                    mm = pe.matmul(p_flat[b], ones_b[:], ctx_q[:, b * NC + c, :], start=(c == 0), stop=(c == NC - 1))
                mm.then_inc(t_col, 1)
            for t in range(NT):
                pe.wait_ge(t_q1, t + 1)
                if t >= 2:
                    pe.wait_ge(t_q1t_out, t - 1)
                for c in range(NC):
                    mm = pe.transpose(p_flat[2 + t % 2].bitcast(BF16)[:, c * P:(c + 1) * P],
                                      q1[:, t, c * P:(c + 1) * P], ident_b[:])
                mm.then_inc(t_q1t, 1)
                if t >= 1:
                    quant_product(pe, t - 1)
            quant_product(pe, NT - 1)
            for t in range(NT):
                pe.wait_ge(t_xn, NT + t + 1)
                for c in range(NC):
                    mm = pe.transpose(acc[t][:, c * P:(c + 1) * P], xn[:, t, c * P:(c + 1) * P], ident[:])
                mm.then_inc(t_x3t, 1)
                if t >= 1:
                    low_rank(pe, t - 1)
            low_rank(pe, NT - 1)
            for t in range(NT):
                base_out(pe, t)
            for t in range(NT):
                pe.wait_ge(t_hw, t + 1)
                pe.transpose(acc[t][:, 0:P], hw[:, t, :], ident[:]).then_inc(t_hwt, 1)
            pe.wait_ge(t_lo, 2)
            for t in range(NT):
                pe.wait_ge(t_hwlo, t + 1)
                y = p_flat[t]
                pe.matmul(y, hwt_hi[:, t, :], bm_hi[:], start=False, stop=False, skip_group_check=True)
                pe.matmul(y, hwt_lo[:, t, :], bm_hi[:], start=False, stop=False, skip_group_check=True)
                pe.matmul(y, hwt_hi[:, t, :], bm_lo[:], start=False, stop=True, skip_group_check=True
                          ).then_inc(t_y, 1)

        @block.scalar
        def _(act):
            for t in range(NT):
                act.wait_ge(xt_ready, t + 1)
                act.copy(xnt_hi[:, :, t * P:(t + 1) * P], acc[t][:].rearrange("p (c n) -> p c n", c=NC)
                         ).then_inc(xt_hi, 1)

            def weights_hi(i, r, before, landed):
                u = before + 4 * i + r
                act.wait_ge(w_landed[r], 16 * (landed + i + 1))
                if not (isinstance(u, int) and u < 2):
                    act.wait_ge(proj_ready, u - 1)
                act.copy(w_hi[:, r % 2, 0:NC * DH], raw[:, r, :]).then_inc(w_hi_done, 1)

            def take(i, r, before, dst, bias):
                u = before + 4 * i + r
                act.wait_ge(proj_ready, u + 1)
                if not (isinstance(u, int) and u < 2):
                    act.wait_ge(summed, u - 1)
                h = 4 * i + r
                act.activation(head(dst, h), acc[r % 2][:], ACT.Identity, bias=column(bias, h))
                act.activation(square[:, r % 2, :], acc[r % 2][:], ACT.Square, bias=column(bias, h)
                               ).then_inc(squared, 1)

            act.wait_ge(const_landed, 16 * 5)
            for r in range(2):
                weights_hi(0, r, 0, 0)
            for r in range(2, 4):
                weights_hi(0, r, 0, 0)
                take(0, r - 2, 0, k_all, bk_c)
            with act.Fori(1, NH // 4) as i:
                for r in range(4):
                    weights_hi(i, r, 0, 0)
                    take(i if r >= 2 else i - 1, (r - 2) % 4, 0, k_all, bk_c)
            for r in range(4):
                weights_hi(0, r, NH, NH // 4)
                if r < 2:
                    take(NH // 4 - 1, r + 2, 0, k_all, bk_c)
                else:
                    take(0, r - 2, NH, q_all, bq_c)
            with act.Fori(1, NH // 4) as i:
                for r in range(4):
                    weights_hi(i, r, NH, NH // 4)
                    take(i if r >= 2 else i - 1, (r - 2) % 4, NH, q_all, bq_c)

            def pair_weights_hi(n, buf, half_, landed):
                act.wait_ge(w_landed[n], 16 * (NH // 2 + landed))
                act.copy(w_hi[:, buf, half_ * 512:(half_ + 1) * 512], raw[:, n, :]).then_inc(w_hi_done, 1)

            def split_k_hi(h):
                act.copy(k_hi[:], head(k_all, h)).then_inc(kq_hi, 1)

            def split_q_hi(h):
                act.copy(q_hi[:], head(q_all, h)).then_inc(kq_hi, 1)

            def v_half_hi(pair, e, par):
                act.wait_ge(v_ready, 2 * pair + e + 1)
                act.copy(v_hi[:, par, 2 * e:2 * e + 2, :], p_v[:]).then_inc(v_hi_done, 1)

            def exps(h, b):
                s = 2 * h + b
                act.wait_ge(nb_done, s + 1)
                for a in range(2):
                    act.activation(probs[:, b, a, :], p_s[:, a, :], ACT.Exp, bias=nbias[:, b, a:a + 1],
                                   scale=rq_t[:, 2 * b + a:2 * b + a + 1], accum_out=rsum[:, b, a:a + 1]
                                   ).then_inc(exp_done, 1)

            act.wait_ge(k_normed, 1)
            split_k_hi(0)
            act.wait_ge(squared, NH + 1)
            split_q_hi(0)
            act.wait_ge(proj_ready, U1 - 1)
            pair_weights_hi(0, 0, 0, 1)
            pair_weights_hi(1, 0, 1, 1)
            take(NH // 4 - 1, 2, NH, q_all, bq_c)
            take(NH // 4 - 1, 3, NH, q_all, bq_c)
            pair_weights_hi(0, 1, 0, 2)
            v_half_hi(0, 0, 0)
            pair_weights_hi(1, 1, 1, 2)
            v_half_hi(0, 1, 0)
            exps(0, 0)

            def pair(p, par, last=False):
                for j in range(4):
                    b = j % 2
                    h = 2 * p + j // 2
                    s = 2 * h + b
                    if b == 0 and not (isinstance(h, int) and h == 0):
                        act.wait_ge(pv_done, 2 * h)
                        act.activation(o_hi[:], p_o[:], ACT.Identity, bias=column(bv_c, h - 1)
                                       ).then_inc(o_hi_done, 1)
                    if b == 0 and not (last and j == 2):
                        act.wait_ge(scores_ready, 2 * h + 2)
                        split_k_hi(h + 1)
                        split_q_hi(h + 1)
                    act.wait_ge(pt_ready, s + 1)
                    act.copy(pt_hi[:], p_t[:]).then_inc(pt_hi_done, 1)
                    if not (last and j == 3):
                        exps(h + b, 1 - b)
                    if b == 1 and not last:
                        v_half_hi(p + 1, j // 2, 1 - par)
                    if b == 1:
                        act.wait_ge(w_landed[1], 16 * (NH // 2 + 3 + 2 * p + j // 2))
                        if not (isinstance(h, int) and h == 0):
                            act.wait_ge(wo_used, h)
                        act.copy(wo_hi[:], raw[:, 1, :]).then_inc(w_hi_done, 1)
                    else:
                        pair_weights_hi(0, par, j // 2, 3 + 2 * p + j // 2)

            pair(0, 0)
            with act.Fori(0, (NP - 2) // 2) as i:
                pair(2 * i + 1, 1)
                pair(2 * i + 2, 0)
            pair(NP - 1, 1, last=True)
            act.wait_ge(pv_done, NS)
            act.activation(o_hi[:], p_o[:], ACT.Identity, bias=bv_c[:, NH - 1:NH]).then_inc(o_hi_done, 1)

            act.wait_ge(tail_landed[2], 16)
            act.copy(ra_hi[:], ra_f[:]).then_inc(t_hi, 1)
            act.wait_ge(tail_landed[4], 16)
            act.copy(bm_hi[:], bm_f[:]).then_inc(t_hi, 1)
            for t in range(NT):
                act.wait_ge(t_xn, t + 1)
                act.activation(xn[:, t, :], xn[:, t, :], ACT.Identity, bias=qs_b[:, 1:2], scale=qc[:, 0:1]
                               ).then_inc(t_lin, 1)
            for t in range(NT):
                act.wait_ge(t_q1t, t + 1)
                act.copy(q1t[:, t, :, :].rearrange("p c n -> p (c n)"), p_flat[2 + t % 2].bitcast(BF16)[:, 0:D]
                         ).then_inc(t_q1t_out, 1)
            for t in range(NT):
                act.wait_ge(t_x3t, t + 1)
                act.copy(xnt_hi[:, :, t * P:(t + 1) * P], acc[t][:].rearrange("p (c n) -> p c n", c=NC)
                         ).then_inc(t_x3hi, 1)
            for t in range(NT):
                act.wait_ge(t_nmax, t + 1)
                act.activation(pr[:, t, :], logit[:, t, :], ACT.Exp, bias=fsm[:, t, 0:1], accum_out=fsm[:, t, 1:2]
                               ).then_inc(t_exp, 1)
            for t in range(NT):
                act.wait_ge(t_hwt, t + 1)
                act.copy(hwt_hi[:, t, :], acc[t][:, 0:P]).then_inc(t_hwhi, 1)

        @block.gpsimd
        def _(pool):
            made = sem("made")
            pool.memset(ident[:], 0.0).then_inc(made, 1)
            pool.memset(mhalf[:], -0.5).then_inc(made, 1)
            pool.memset(ones[:], 1.0).then_inc(made, 1)
            pool.memset(acc_k[:], 0.0).then_inc(made, 1)
            pool.memset(acc_q[:], 0.0).then_inc(made, 1)
            pool.wait_ge(made, 5)
            pool.affine_select(out=ident[:], in_=ident[:], compare_op=ALU.not_equal, fill=1.0, base=0,
                               pattern=[[-1, P]], channel_multiplier=1).then_inc(consts_made, 1)
            for t in range(NT):
                pool.wait_ge(ln_var, t + 1)
                pool.tensor_tensor(rstd[:, t:t + 1], vare[:, t:t + 1], mhalf[:, t:t + 1], ALU.pow
                                   ).then_inc(gpow, 1)
            pool.wait_ge(consts_made, 1)
            pool.tensor_copy(ident_b[:], ident[:]).then_inc(consts_made, 1)

            def add_square(i, r, before, sums):
                u = before + 4 * i + r
                pool.wait_ge(squared, u + 1)
                if not (isinstance(u, int) and u == 0):
                    pool.wait_ge(summed, u)
                pool.tensor_tensor(sums[:], sums[:], square[:, r % 2, :], ALU.add).then_inc(summed, 1)

            for r in range(4):
                add_square(0, r, 0, acc_k)
            with pool.Fori(1, NH // 4) as i:
                for r in range(4):
                    add_square(i, r, 0, acc_k)
            pool.wait_ge(ssq_out, 1)
            pool.tensor_tensor(rk_t[:], ssq[:], mhalf[:], ALU.pow).then_inc(rms_pow, 1)
            for r in range(4):
                add_square(0, r, NH, acc_q)
            with pool.Fori(1, NH // 4) as i:
                for r in range(4):
                    add_square(i, r, NH, acc_q)

            def chunk_lo(dst, hi, slot, n):
                pool.wait_ge(w_hi_done, U1 + n + 1)
                pool.tensor_tensor(dst, raw[:, slot, :], hi, ALU.subtract).then_inc(w_lo_pool, 1)

            def pair_chunk_lo(buf, half_, slot, n):
                cols = slice(half_ * 512, (half_ + 1) * 512)
                chunk_lo(w_lo[:, buf, cols], w_hi[:, buf, cols], slot, n)

            def split_kq_lo(h):
                pool.wait_ge(kq_hi, 2 * h + 1)
                pool.tensor_tensor(k_lo[:], head(k_all, h), k_hi[:], ALU.subtract).then_inc(kq_lo, 1)
                pool.wait_ge(kq_hi, 2 * h + 2)
                pool.tensor_tensor(q_lo[:], head(q_all, h), q_hi[:], ALU.subtract).then_inc(kq_lo, 1)

            pool.wait_ge(ssq_out, 2)
            pool.tensor_tensor(rq_t[:], ssq[:], mhalf[:], ALU.pow).then_inc(rms_pow, 1)

            def pair(p, par, last=False):
                for j in range(4):
                    h = 2 * p + j // 2
                    if j % 2 == 0 and not (last and j == 2):
                        split_kq_lo(h + 1)
                    if j % 2:
                        chunk_lo(wo_lo[:], wo_hi[:], 1, 4 + 4 * p + j)
                    else:
                        pair_chunk_lo(par, j // 2, 0, 4 + 4 * p + j)

            pair(0, 0)
            with pool.Fori(0, (NP - 2) // 2) as i:
                pair(2 * i + 1, 1)
                pair(2 * i + 2, 0)
            pair(NP - 1, 1, last=True)

            pool.memset(ones_b[:], 1.0).then_inc(t_ones, 1)
            pool.wait_ge(t_hi, 1)
            pool.tensor_tensor(ra_lo[:], ra_f[:], ra_hi[:], ALU.subtract).then_inc(t_lo, 1)
            pool.wait_ge(t_hi, 2)
            pool.tensor_tensor(bm_lo[:], bm_f[:], bm_hi[:], ALU.subtract).then_inc(t_lo, 1)
            for t in range(2 * NT):
                pool.wait_ge(t_var, t + 1)
                pool.tensor_tensor(rstd[:, t % NT:t % NT + 1], vare[:, t % NT:t % NT + 1],
                                   mhalf[:, 0:1], ALU.pow).then_inc(t_pow, 1)

        @block.vector
        def _(dve):
            links = 0

            def link(ins):
                nonlocal links
                links += 1
                ins.then_inc(chain, 1)
                dve.wait_ge(chain, links)

            def variance(src, t, ready):
                link(dve.bn_stats(stats[:, t, :], src))
                link(dve.bn_aggr(mv[:, t, :], stats[:, t, :]))
                dve.tensor_scalar(vare[:, t:t + 1], mv[:, t, 1:2], EPS_LN, None, ALU.add).then_inc(ready, 1)

            for t in range(NT):
                dve.wait_ge(x_landed[t], 16)
                variance(xin[:, t, :], t, ln_var)
                if t >= 1:
                    dve.wait_ge(gpow, t)
                    dve.tensor_scalar(xin[:, t - 1, :], xin[:, t - 1, :], mv[:, t - 1, 0:1], rstd[:, t - 1:t],
                                      ALU.subtract, ALU.mult).then_inc(ln_done, 1)
            dve.wait_ge(gpow, NT)
            dve.tensor_scalar(xin[:, NT - 1, :], xin[:, NT - 1, :], mv[:, NT - 1, 0:1], rstd[:, NT - 1:NT],
                              ALU.subtract, ALU.mult).then_inc(ln_done, 1)
            for t in range(NT):
                dve.wait_ge(xt_hi, t + 1)
                tt = slice(t * P, (t + 1) * P)
                dve.tensor_tensor(xnt_lo[:, :, tt], acc[t][:].rearrange("p (c n) -> p c n", c=NC),
                                  xnt_hi[:, :, tt], ALU.subtract).then_inc(xt_lo, 1)

            def weights_lo(i, r, before):
                dve.wait_ge(w_hi_done, before + 4 * i + r + 1)
                n = r % 2
                dve.tensor_tensor(w_lo[:, n, 0:NC * DH], raw[:, r, :], w_hi[:, n, 0:NC * DH], ALU.subtract
                                  ).then_inc(w_lo_dve, 1)

            def norm_k(i, r):
                h = 4 * i + r
                dve.scalar_tensor_tensor(out=head(k_all, h), in0=head(k_all, h), scalar=column(g_c, h),
                                         in1=rkb[:], op0=ALU.mult, op1=ALU.mult).then_inc(k_normed, 1)

            for r in range(4):
                weights_lo(0, r, 0)
            dve.wait_ge(const_landed, 16 * 5)
            link(dve.scalar_tensor_tensor(out=g_c[:], in0=g_c[:], scalar=float(DH) ** -0.5, in1=gq_c[:],
                                          op0=ALU.mult, op1=ALU.mult))
            with dve.Fori(1, NH // 4) as i:
                for r in range(4):
                    weights_lo(i, r, 0)

            def mean_squares(src, n):
                dve.wait_ge(ssq_ready, n)
                dve.tensor_scalar(ssq[:], src[:, 0:NT], 1.0 / INNER, EPS_RMS, ALU.mult, ALU.add
                                  ).then_inc(ssq_out, 1)

            weights_lo(0, 0, NH)
            weights_lo(0, 1, NH)
            mean_squares(p_flat[0], 1)
            weights_lo(0, 2, NH)
            dve.wait_ge(rms_pow, 1)
            for t in range(NT):
                dve.tensor_scalar(diag[:, t, :], ident[:], rk_t[:, t:t + 1], None, ALU.mult).then_inc(diag_made, 1)
            weights_lo(0, 3, NH)
            dve.wait_ge(rkb_ready, 1)
            link(dve.tensor_copy(rkb[:], p_flat[1]))
            for r in range(4):
                norm_k(0, r)
            with dve.Fori(1, NH // 4) as i:
                for r in range(4):
                    weights_lo(i, r, NH)
                    norm_k(i, r)

            def slot_max(h, b):
                s = 2 * h + b
                dve.wait_ge(scores_ready, s + 1)
                dve.tensor_reduce(nmax[:, b, :], p_s[:], AX.X, ALU.max, negate=True).then_inc(max_done, 1)
                dve.wait_ge(max_done, s + 1)
                dve.tensor_tensor(nbias[:, b, :], nmax[:, b, :], rq_t[:, 2 * b:2 * b + 2], ALU.mult
                                  ).then_inc(nb_done, 1)

            def slot_norm(h, b):
                s = 2 * h + b
                dve.wait_ge(exp_done, 2 * s + 2)
                dve.reciprocal(rinv[:, b, :], rsum[:, b, :]).then_inc(rinv_done, 1)
                dve.wait_ge(rinv_done, s + 1)
                dve.tensor_scalar(probs[:, b, 0, :], probs[:, b, 0, :], rinv[:, b, 0:1], None, ALU.mult)
                dve.tensor_scalar(probs[:, b, 1, :], probs[:, b, 1, :], rinv[:, b, 1:2], None, ALU.mult
                                  ).then_inc(p_normed, 1)

            def v_half_lo(pair, e, par):
                dve.wait_ge(v_hi_done, 2 * pair + e + 1)
                dve.tensor_tensor(v_lo[:, par, 2 * e:2 * e + 2, :], p_v[:], v_hi[:, par, 2 * e:2 * e + 2, :],
                                  ALU.subtract).then_inc(v_lo_done, 1)

            def out_lo(h):
                dve.wait_ge(o_hi_done, h + 1)
                dve.scalar_tensor_tensor(out=o_lo[:], in0=p_o[:], scalar=column(bv_c, h), in1=o_hi[:],
                                         op0=ALU.add, op1=ALU.subtract).then_inc(o_lo_done, 1)

            def first_pairs_lo(n):
                dve.wait_ge(w_hi_done, U1 + n + 1)
                cols = slice(n % 2 * 512, n % 2 * 512 + 512)
                dve.tensor_tensor(w_lo[:, n // 2, cols], raw[:, n % 2, :], w_hi[:, n // 2, cols], ALU.subtract
                                  ).then_inc(w_lo_dve, 1)

            dve.wait_ge(kq_hi, 2)
            dve.tensor_tensor(k_lo[:], k_all[:, 0, :], k_hi[:], ALU.subtract).then_inc(kq_lo, 1)
            dve.tensor_tensor(q_lo[:], q_all[:, 0, :], q_hi[:], ALU.subtract).then_inc(kq_lo, 1)
            first_pairs_lo(0)
            first_pairs_lo(1)
            first_pairs_lo(2)
            v_half_lo(0, 0, 0)
            mean_squares(p_flat[2], 2)
            first_pairs_lo(3)
            dve.wait_ge(rms_pow, 2)
            slot_max(0, 0)
            v_half_lo(0, 1, 0)
            slot_norm(0, 0)

            def pair(p, par, last=False, extra=None):
                for j in range(4):
                    b = j % 2
                    h = 2 * p + j // 2
                    s = 2 * h + b
                    end = last and j == 3
                    if not end:
                        slot_max(h + b, 1 - b)
                    if b == 0 and not (isinstance(h, int) and h == 0):
                        out_lo(h - 1)
                    dve.wait_ge(pt_hi_done, s + 1)
                    dve.tensor_tensor(pt_lo[:], p_t[:], pt_hi[:], ALU.subtract).then_inc(pt_lo_done, 1)
                    if not end:
                        slot_norm(h + b, 1 - b)
                    if b == 1 and not last:
                        v_half_lo(p + 1, j // 2, 1 - par)
                    if extra:
                        extra(j)

            def quantise_ctx(j):
                a = slice(2 * j, 2 * j + 2)
                c = ctx_f[:, a, :]
                link(dve.tensor_scalar(c, c, qc[:, 1:2], qs_b[:, 3:4], ALU.mult, ALU.add))
                link(dve.tensor_scalar(c, c, QMIN, QMAX, ALU.max, ALU.min))
                dve.tensor_scalar(ctx_q[:, a, :], c, ROUND, ROUND + MID, ALU.add, ALU.subtract).then_inc(t_ctxq, 1)

            pair(0, 0)
            with dve.Fori(0, (NP - 2) // 2) as i:
                pair(2 * i + 1, 1)
                pair(2 * i + 2, 0)
            dve.wait_ge(tail_landed[0], 16)
            link(dve.reciprocal(qc[:, 0:1], qs_b[:, 0:1]))
            link(dve.reciprocal(qc[:, 1:2], qs_b[:, 2:3]))
            link(dve.tensor_tensor(qc[:, 2:3], qs_b[:, 0:1], qs_b[:, 2:3], ALU.mult))
            link(dve.tensor_scalar(qc[:, 3:4], qs_b[:, 1:2], -1.0, MID, ALU.mult, ALU.add))
            link(dve.tensor_scalar(qc[:, 4:5], qs_b[:, 3:4], -1.0, MID, ALU.mult, ALU.add))
            link(dve.tensor_scalar(qc[:, 5:7], qc[:, 3:5], qc[:, 2:3], None, ALU.mult))
            dve.wait_ge(tail_landed[1], 16)
            pair(NP - 1, 1, last=True, extra=quantise_ctx)
            out_lo(NH - 1)

            dve.wait_ge(tail_landed[3], 16 * (NT + 1))
            for t in range(NT):
                link(dve.tensor_tensor(x_res[:, t, :], x_res[:, t, :], bo_b[:], ALU.add))
            link(dve.tensor_scalar(sc[:, 0:1], qc[:, 4:5], float(D), None, ALU.mult))
            for b in range(B):
                dve.wait_ge(t_col, b + 1)
                dve.tensor_scalar(corr[:, b, :], p_flat[b], sc[:, 0:1], qc[:, 5:6], ALU.add, ALU.mult
                                  ).then_inc(t_corr, 1)
            dve.wait_ge(wo_used, NH)

            def normalise(t, n):
                dve.wait_ge(t_pow, n)
                dve.tensor_scalar(xn[:, t, :], x_res[:, t, :], mv[:, t, 0:1], rstd[:, t:t + 1],
                                  ALU.subtract, ALU.mult).then_inc(t_xn, 1)

            def quantise(t):
                dve.wait_ge(t_lin, t + 1)
                link(dve.tensor_scalar(xn[:, t, :], xn[:, t, :], QMIN, QMAX, ALU.max, ALU.min))
                dve.tensor_scalar(q1[:, t, :], xn[:, t, :], ROUND, ROUND + MID, ALU.add, ALU.subtract
                                  ).then_inc(t_q1, 1)

            for t in range(NT):
                dve.tensor_tensor(x_res[:, t, :], acc[t][:], x_res[:, t, :], ALU.add).then_inc(t_x1, 1)
                dve.wait_ge(t_x1, t + 1)
                variance(x_res[:, t, :], t, t_var)
                if t >= 1:
                    normalise(t - 1, t)
                if t >= 2:
                    quantise(t - 2)
            normalise(NT - 1, NT)
            quantise(NT - 2)
            quantise(NT - 1)
            for t in range(NT):
                b = t // 2
                dve.wait_ge(t_qq, t + 1)
                link(dve.tensor_scalar(rsd[:, t:t + 1], p_flat[t % 2][:, 0:1], qc[:, 6:7], None, ALU.mult))
                link(dve.scalar_tensor_tensor(out=xn[:, t, :], in0=acc[t][:],
                                              scalar=qc[:, 2:3], in1=corr[:, b, :], op0=ALU.mult, op1=ALU.add))
                dve.scalar_tensor_tensor(out=x_res[:, t, :], in0=xn[:, t, :], scalar=rsd[:, t:t + 1],
                                         in1=x_res[:, t, :], op0=ALU.add, op1=ALU.add).then_inc(t_x2, 1)
                dve.wait_ge(t_x2, t + 1)
                variance(x_res[:, t, :], t, t_var)
                if t >= 1:
                    normalise(t - 1, NT + t)
            normalise(NT - 1, 2 * NT)
            dve.wait_ge(tail_landed[5], 16)
            dve.wait_ge(tail_landed[6], 16)
            dve.wait_ge(tail_landed[7], 16)
            link(dve.tensor_copy(emf[:], em_i[:]))
            for e in range(NE):
                link(dve.tensor_scalar(onehot[:, e, :], emf[:], float(e), None, ALU.is_equal))
            for t in range(NT):
                dve.wait_ge(t_x3hi, t + 1)
                tt = slice(t * P, (t + 1) * P)
                dve.tensor_tensor(xnt_lo[:, :, tt], acc[t][:].rearrange("p (c n) -> p c n", c=NC),
                                  xnt_hi[:, :, tt], ALU.subtract).then_inc(t_x3lo, 1)
            for t in range(NT):
                link(dve.tensor_tensor(x_res[:, t, :], x_res[:, t, :], bb_b[:], ALU.add))
            for t in range(NT):
                dve.wait_ge(t_ra, t + 1)
                link(dve.tensor_tensor(logit[:, t, :], acc[t][:, P:P + NR], rb_b[:], ALU.add))
                dve.tensor_reduce(fsm[:, t, 0:1], logit[:, t, :], AX.X, ALU.max, negate=True).then_inc(t_nmax, 1)
            for t in range(NT):
                dve.wait_ge(t_exp, t + 1)
                link(dve.reciprocal(fsm[:, t, 2:3], fsm[:, t, 1:2]))
                link(dve.tensor_scalar(pr[:, t, :], pr[:, t, :], fsm[:, t, 2:3], None, ALU.mult))
                link(dve.max(out=top8[:, t, :], in_=pr[:, t, :]))
                link(dve.match_replace(out=cut[:, t, :], in_to_replace=top8[:, t, :], in_values=pr[:, t, :],
                                       imm_value=-1.0))
                link(dve.scalar_tensor_tensor(out=kept[:, t, :], in0=cut[:, t, :], scalar=0.0, in1=pr[:, t, :],
                                              op0=ALU.is_lt, op1=ALU.mult))
                link(dve.tensor_tensor(spread[:, t, :, :], kept[:, t, :].unsqueeze(1).to_broadcast([P, NE, NR]),
                                       onehot[:], ALU.mult))
                link(dve.tensor_reduce(gate[:, t, :], spread[:, t, :, :], AX.X, ALU.add))
                dve.scalar_tensor_tensor(out=hw[:, t, :].rearrange("p (e r) -> p e r", e=NE),
                                         in0=acc[t][:, 0:P].rearrange("p (e r) -> p e r", e=NE), scalar=2.0,
                                         in1=gate[:, t, :].unsqueeze(2).to_broadcast([P, NE, RK]),
                                         op0=ALU.mult, op1=ALU.mult).then_inc(t_hw, 1)
            for t in range(NT):
                dve.wait_ge(t_hwhi, t + 1)
                dve.tensor_tensor(hwt_lo[:, t, :], acc[t][:, 0:P], hwt_hi[:, t, :], ALU.subtract
                                  ).then_inc(t_hwlo, 1)
            for t in range(NT):
                dve.wait_ge(t_y, t + 1)
                dve.tensor_tensor(xn[:, t, :], p_flat[t], x_res[:, t, :], ALU.add).then_inc(t_out, 1)


def kernel(**inputs):
    import numpy as np
    from concourse import bacc
    from concourse.bass_utils import run_bass_kernel_spmd

    a = {k: np.asarray(v) for k, v in inputs.items()}

    def per_head(w):
        return np.ascontiguousarray(w.reshape(NC, P, NH, DH).transpose(2, 1, 0, 3)).reshape(NH, P, NC * DH)

    def per_pair(w):
        n = w.shape[1] // PW
        t = w.reshape(2, 2, P, n, PW).transpose(3, 0, 2, 1, 4)
        return np.ascontiguousarray(t).reshape(2 * n, P, 2 * PW)

    def columns(v):
        return np.ascontiguousarray(v.reshape(NH, DH).T)

    wv_base = np.concatenate([a["L0_attn_Wv"], a["L0_ffn_base_W"].T], axis=1)
    a_r = np.concatenate([a["L0_ffn_A"].reshape(NE * RK, D), a["L0_ffn_router_W"],
                          np.zeros((1, D), np.float32)], axis=0)
    arrays = {
        "in_x": a["x"].reshape(NT, P, D),
        "in_ctx": np.ascontiguousarray(a["ctx_4096"].reshape(B * NC, P, SKV).transpose(1, 0, 2)),
        "in_wk": per_head(a["L0_attn_Wk"]),
        "in_wq": per_head(a["L0_attn_Wq"]),
        "in_wv": per_pair(wv_base),
        "in_wo": a["L0_attn_Wo"].reshape(NH, DH, D),
        "in_bk": columns(a["L0_attn_bk"]),
        "in_bq": columns(a["L0_attn_bq"]),
        "in_bv": columns(a["L0_attn_bv"]),
        "in_bo": a["L0_attn_bo"],
        "in_gk": columns(a["L0_attn_gk"]),
        "in_gq": columns(a["L0_attn_gq"]),
        "in_qs": np.concatenate([a["L0_xattn_x1_scale"], a["L0_xattn_x1_zp"], a["L0_xattn_x2_scale"],
                                 a["L0_xattn_x2_zp"]]),
        "in_ra": np.ascontiguousarray(a_r.T.reshape(NC, P, RA).transpose(1, 0, 2)).reshape(P, NC * RA),
        "in_bb": a["L0_ffn_base_b"],
        "in_rb": a["L0_ffn_router_b"],
        "in_bm": np.ascontiguousarray(a["L0_ffn_B"].transpose(0, 2, 1)).reshape(NE * RK, D),
        "in_em": a["L0_ffn_expert_map"],
    }
    nc = bacc.Bacc("TRN2", target_bir_lowering=False, num_devices=1)
    args = [nc.dram_tensor(k, v.shape, mybir.dt.from_np(v.dtype), kind="ExternalInput").ap()
            for k, v in arrays.items()]
    y = nc.dram_tensor("out_y", (NT, P, D), F32, kind="ExternalOutput").ap()
    decoder_layer(nc, *args, y)
    r = run_bass_kernel_spmd(nc, [arrays], core_ids=[0])
    return r.results[0]["out_y"].reshape(B, S, D)
```

```python
from contextlib import ExitStack

import concourse.bass as bass
from concourse import mybir

F32 = mybir.dt.float32
F32R = mybir.dt.float32r
BF16 = mybir.dt.bfloat16
I32 = mybir.dt.int32
ALU = mybir.AluOpType
ACT = mybir.ActivationFunctionType
AX = mybir.AxisListType

P = 128
B, S, D = 2, 256, 512
T = B * S
NT = T // P
NC = D // P
SKV = 512
NH, DH = 32, 128
NP = NH // 2
NS = 2 * NH
PW = 2 * DH
INNER = NH * DH
NE, RK, NR = 8, 16, 15
RA = P + NR + 1
EPS_LN, EPS_RMS = 1e-5, 1e-6
ROUND = 12582912.0
MID = 128.0
QMIN, QMAX = 0.0, 255.0
U1 = 2 * NH


def decoder_layer(nc, x, ctx_t, wk, wq, wv, wo, bk, bq, bv, bo, gk, gq, qscal, ra_w, base_b, router_b, bm_w,
                  expert_map, out):
    st = ExitStack()
    with st:
        def sem(name):
            return st.enter_context(nc.semaphore(name))

        def bank(name, shape, dt=F32):
            return st.enter_context(nc.psum_tensor(name, shape, dt))

        base = (nc.sbuf_base + 63) // 64 * 64
        top = [base]

        def place(name, shape, dt, at=None):
            size = {F32: 4, F32R: 4, BF16: 2, I32: 4}[dt]
            for n in shape[1:]:
                size *= n
            if at is None:
                at = top[0]
                top[0] += (size + 31) // 32 * 32
            return nc.alloc_sbuf_tensor_at(name, shape, dt, offset=at), at

        def here(name, shape, dt, at=None):
            return place(name, shape, dt, at)[0]

        xnt_hi = here("xnt_hi", [P, NC, T], F32R)
        xnt_lo = here("xnt_lo", [P, NC, T], F32R)
        k_all, k_at = place("k_all", [P, NH, T], F32)
        q_all, q_at = place("q_all", [P, NH, T], F32)
        v_hi, vh_at = place("v_hi", [P, 2, NT, PW], F32R)
        v_lo, vl_at = place("v_lo", [P, 2, NT, PW], F32R)
        k_hi, kh_at = place("k_hi", [P, T], F32R)
        k_lo, kl_at = place("k_lo", [P, T], F32R)
        q_hi, qh_at = place("q_hi", [P, T], F32R)
        q_lo, ql_at = place("q_lo", [P, T], F32R)
        pt_hi, pt_at = place("pt_hi", [P, 2, S], F32R)
        pt_lo = here("pt_lo", [P, 2, S], F32R)
        o_hi = here("o_hi", [P, T], F32R)
        o_lo = here("o_lo", [P, T], F32R)
        wo_hi = here("wo_hi", [P, D], F32R)
        wo_lo = here("wo_lo", [P, D], F32R)
        raw, raw_at = place("raw", [P, 4, 512], F32)
        probs = here("probs", [P, 2, 2, S], F32, raw_at + 2 * 2048)
        w_hi = here("w_hi", [P, 2, NC * PW], F32R)
        w_lo = here("w_lo", [P, 2, NC * PW], F32R)
        ident = here("ident", [P, P], F32)
        ident_b = here("ident_b", [P, P], BF16)
        ones = here("ones", [P, P], F32)
        bk_c = here("bk_c", [P, NH], F32)
        bq_c = here("bq_c", [P, NH], F32)
        bv_c = here("bv_c", [P, NH], F32)
        g_c = here("g_c", [P, NH], F32)
        gq_c = here("gq_c", [P, NH], F32)
        mhalf = here("mhalf", [P, NT], F32)
        ssq = here("ssq", [P, NT], F32)
        rk_t = here("rk_t", [P, NT], F32)
        rq_t = here("rq_t", [P, NT], F32)
        nmax = here("nmax", [P, 2, 2], F32)
        nbias = here("nbias", [P, 2, 2], F32)
        rsum = here("rsum", [P, 2, 2], F32)
        rinv = here("rinv", [P, 2, 2], F32)
        stats = here("stats", [P, NT, 6], F32)
        mv = here("mv", [P, NT, 2], F32)
        vare = here("vare", [P, NT], F32)
        rstd = here("rstd", [P, NT], F32)
        sc = here("sc", [P, 8], F32)
        assert top[0] <= nc.sbuf_usable_end, (top[0], nc.sbuf_usable_end)

        half = NT * PW * 4
        acc_k = here("acc_k", [P, T], F32, vh_at + half)
        acc_q = here("acc_q", [P, T], F32, vh_at + half + 2048)
        rkb = here("rkb", [P, T], F32, vl_at + half)
        diag = here("diag", [P, NT, P], F32, vl_at + half + 2048)
        square = here("square", [P, 2, T], F32, pt_at)
        xin = here("xin", [P, NT, D], F32, q_at + (NH - NT) * T * 4)
        KS = T * 4
        x_res = here("x_res", [P, NT, D], F32, k_at)
        ctx_f = here("ctx_f", [P, B * NC, SKV], F32, k_at + 4 * KS)
        rb_b = here("rb_b", [P, NR], F32, k_at + 12 * KS)
        em_i = here("em_i", [P, NR], I32, k_at + 12 * KS + 64)
        qs_b = here("qs_b", [P, 4], F32, k_at + 12 * KS + 128)
        bo_b = here("bo_b", [P, D], F32, k_at + 13 * KS)
        bb_b = here("bb_b", [P, D], F32, k_at + 14 * KS)
        bm_f = here("bm_f", [P, D], F32, k_at + 15 * KS)
        ra_f = here("ra_f", [P, NC * RA], F32, k_at + 16 * KS)
        ctx_q = here("ctx_q", [P, B * NC, SKV], BF16, k_at + 18 * KS)
        xn = here("xn", [P, NT, D], F32, q_at)
        q1 = here("q1", [P, NT, D], BF16, q_at + 4 * KS)
        q1t = here("q1t", [P, NT, NC, P], BF16, q_at + 6 * KS)
        corr = here("corr", [P, B, SKV], F32, q_at + 8 * KS)
        hw = here("hw", [P, NT, P], F32, q_at + 10 * KS)
        ones_b = here("ones_b", [P, P], BF16, q_at + 11 * KS)
        small_at = q_at + 12 * KS
        emf = here("emf", [P, NR], F32, small_at)
        onehot = here("onehot", [P, NE, NR], F32, small_at + 128)
        logit = here("logit", [P, NT, NR], F32, small_at + 1024)
        pr = here("pr", [P, NT, NR], F32, small_at + 1536)
        top8 = here("top8", [P, NT, 8], F32, small_at + 2048)
        cut = here("cut", [P, NT, NR], F32, small_at + 2304)
        kept = here("kept", [P, NT, NR], F32, small_at + 2560)
        spread = here("spread", [P, NT, NE, NR], F32, small_at + 3072)
        gate = here("gate", [P, NT, NE], F32, small_at + 5120)
        fsm = here("fsm", [P, 3 * NT], F32, small_at + 5376)
        cs = here("cs", [P, NT], F32, small_at + 5888)
        cm = here("cm", [P, NT], F32, small_at + 5952)
        cb = here("cb", [P, NT], F32, small_at + 6016)
        rsd = here("rsd", [P, NT], F32, small_at + 5632)
        qc = here("qc", [P, 8], F32, small_at + 5760)
        ra_hi = here("ra_hi", [P, NC * RA], F32R, q_at + 16 * KS)
        ra_lo = here("ra_lo", [P, NC * RA], F32R, q_at + 18 * KS)
        bm_hi = here("bm_hi", [P, D], F32R, q_at + 20 * KS)
        bm_lo = here("bm_lo", [P, D], F32R, q_at + 21 * KS)
        wo_last_hi = here("wo_last_hi", [P, D], F32R, q_at + 22 * KS)
        wo_last_lo = here("wo_last_lo", [P, D], F32R, q_at + 23 * KS)
        wo_last_f = here("wo_last_f", [P, D], F32, q_at + 26 * KS)
        o_last_hi = here("o_last_hi", [P, T], F32R, q_at + 24 * KS)
        o_last_lo = here("o_last_lo", [P, T], F32R, q_at + 25 * KS)
        hwt_hi = here("hwt_hi", [P, NT, P], F32R, qh_at)
        hwt_lo = here("hwt_lo", [P, NT, P], F32R, ql_at)

        acc = [bank(f"acc{t}", [P, D]) for t in range(NT)]
        p_v = bank("p_v", [P, 2, PW])
        p_s = bank("p_s", [P, 2, S])
        p_t = bank("p_t", [P, 2, S])
        p_o = bank("p_o", [P, T])
        p_rows = [p_v, p_s, p_t, p_o]
        p_flat = [p_v[:].rearrange("p a b -> p (a b)"), p_s[:].rearrange("p a b -> p (a b)"),
                  p_t[:].rearrange("p a b -> p (a b)"), p_o[:]]

        x_landed = [sem(f"x_landed{t}") for t in range(NT)]
        const_landed = sem("const_landed")
        w_landed = [sem(f"w_landed{r}") for r in range(4)]
        consts_made = sem("consts_made")
        gpow = sem("gpow")
        ln_var = sem("ln_var")
        ln_done = sem("ln_done")
        xt_ready = sem("xt_ready")
        xt_hi = sem("xt_hi")
        xt_lo = sem("xt_lo")
        w_hi_done = sem("w_hi_done")
        w_lo_dve = sem("w_lo_dve")
        w_lo_pool = sem("w_lo_pool")
        proj_ready = sem("proj_ready")
        squared = sem("squared")
        summed = sem("summed")
        ssq_ready = sem("ssq_ready")
        ssq_out = sem("ssq_out")
        rms_pow = sem("rms_pow")
        diag_made = sem("diag_made")
        rkb_ready = sem("rkb_ready")
        rkb_out = sem("rkb_out")
        k_normed = sem("k_normed")
        kq_hi = sem("kq_hi")
        kq_lo = sem("kq_lo")
        scores_ready = sem("scores_ready")
        max_done = sem("max_done")
        nb_done = sem("nb_done")
        exp_done = sem("exp_done")
        rinv_done = sem("rinv_done")
        p_normed = sem("p_normed")
        pt_ready = sem("pt_ready")
        pt_hi_done = sem("pt_hi_done")
        pt_lo_done = sem("pt_lo_done")
        pv_done = sem("pv_done")
        o_hi_done = sem("o_hi_done")
        o_lo_done = sem("o_lo_done")
        v_ready = sem("v_ready")
        v_hi_done = sem("v_hi_done")
        v_lo_done = sem("v_lo_done")
        wo_used = sem("wo_used")
        tail_landed = [sem(f"tail_landed{n}") for n in range(9)]
        stored = sem("stored")
        quarter = sem("quarter")
        chain = sem("chain")
        xb_done = sem("xb_done")
        t_acc = sem("t_acc")
        t_ones = sem("t_ones")
        t_ctxq = sem("t_ctxq")
        t_col = sem("t_col")
        t_corr = sem("t_corr")
        t_var = sem("t_var")
        t_pow = sem("t_pow")
        t_coef = sem("t_coef")
        t_lin = sem("t_lin")
        t_q1 = sem("t_q1")
        t_q1t = sem("t_q1t")
        t_q1t_out = sem("t_q1t_out")
        t_rsd = sem("t_rsd")
        t_qq = sem("t_qq")
        t_tmp = sem("t_tmp")
        t_x2 = sem("t_x2")
        t_xn = sem("t_xn")
        t_xbb = sem("t_xbb")
        t_hi = sem("t_hi")
        t_lo = sem("t_lo")
        t_x3t = sem("t_x3t")
        t_x3hi = sem("t_x3hi")
        t_x3lo = sem("t_x3lo")
        t_ra = sem("t_ra")
        t_sub = sem("t_sub")
        t_exp = sem("t_exp")
        t_onehot = sem("t_onehot")
        t_hw = sem("t_hw")
        t_hwt = sem("t_hwt")
        t_hwhi = sem("t_hwhi")
        t_hwlo = sem("t_hwlo")
        t_y = sem("t_y")
        t_out = sem("t_out")

        def head(a, h):
            return a[:, bass.ds(h, 1), :].rearrange("p a t -> p (a t)")

        def column(a, h):
            return a[:, bass.ds(h, 1)]

        def parts(n):
            return [w[:, n, 0:NC * DH].rearrange("p (c n) -> p c n", c=NC) for w in (w_hi, w_lo)]

        def pair_parts(n):
            return [w[:, n, :].rearrange("p (c n) -> p c n", c=NC) for w in (w_hi, w_lo)]


        block = st.enter_context(nc.Block())

        @block.sync
        def _(sp):
            for t in range(NT):
                sp.dma_start(xin[:, t, :], x[t]).then_inc(x_landed[t], 16)
            for r in range(4):
                sp.dma_start(raw[:, r, :], wk[r]).then_inc(w_landed[r], 16)
            for dst, src in ((bk_c, bk), (bq_c, bq), (bv_c, bv), (g_c, gk), (gq_c, gq)):
                sp.dma_start(dst[:], src).then_inc(const_landed, 16)

            def load_heads(w, i, before):
                for r in range(4):
                    sp.wait_ge(w_lo_dve, before + 4 * i + r - 3)
                    sp.dma_start(raw[:, r, :], w[bass.ds(4 * i + r, 1)].rearrange("a p n -> (a p) n")
                                 ).then_inc(w_landed[r], 16)

            with sp.Fori(1, NH // 4) as i:
                load_heads(wk, i, 0)
            with sp.Fori(0, NH // 4) as i:
                load_heads(wq, i, NH)

            def load_wv(pair, c, n):
                sp.dma_start(raw[:, n, :], wv[bass.ds(2 * pair + c, 1)].rearrange("a p n -> (a p) n")
                             ).then_inc(w_landed[n], 16)

            def load_wo(h):
                sp.dma_start(raw[:, 1, :], wo[bass.ds(h, 1)].rearrange("a p n -> (a p) n")
                             ).then_inc(w_landed[1], 16)

            for n in range(4):
                sp.wait_ge(w_lo_dve, U1 - 3 + n if n < 2 else U1 + n - 1)
                load_wv(n // 2, n % 2, n % 2)

            def pair_loads(p):
                for j in range(3 if isinstance(p, int) and p == NP - 1 else 4):
                    if isinstance(p, int) and p == 0 and j < 2:
                        sp.wait_ge(w_lo_dve, U1 + 3 + j)
                    else:
                        sp.wait_ge(w_lo_pool, 4 * p + j - 1)
                    if j % 2:
                        load_wo(2 * p + j // 2)
                    else:
                        load_wv(p + 2, j // 2, 0)

            pair_loads(0)
            with sp.Fori(1, 8) as p:
                pair_loads(p)
            sp.wait_ge(scores_ready, 2 * 13)
            sp.dma_start(qs_b[:], qscal.partition_broadcast(P)).then_inc(tail_landed[0], 16)
            half_ctx = B * NC // 2
            sp.dma_start(ctx_f[:, 0:half_ctx, :], ctx_t[:, 0:half_ctx, :]).then_inc(tail_landed[1], 16)
            pair_loads(8)
            sp.dma_start(ctx_f[:, half_ctx:, :], ctx_t[:, half_ctx:, :]).then_inc(tail_landed[1], 16)
            pair_loads(9)
            sp.wait_ge(scores_ready, 2 * 18)
            sp.dma_start(bo_b[:], bo.partition_broadcast(P)).then_inc(tail_landed[3], 16)
            for t in range(NT):
                sp.dma_start(x_res[:, t, :], x[t]).then_inc(tail_landed[3], 16)
            pair_loads(10)
            sp.dma_start(ra_f[:], ra_w).then_inc(tail_landed[2], 16)
            sp.dma_start(bm_f[:], bm_w).then_inc(tail_landed[4], 16)
            sp.dma_start(bb_b[:], base_b.partition_broadcast(P)).then_inc(tail_landed[5], 16)
            sp.dma_start(rb_b[:], router_b.partition_broadcast(P)).then_inc(tail_landed[6], 16)
            sp.dma_start(em_i[:], expert_map.partition_broadcast(P)).then_inc(tail_landed[7], 16)
            for p in range(11, NP - 1):
                pair_loads(p)
            sp.dma_start(wo_last_f[:], wo[NH - 1]).then_inc(tail_landed[8], 16)
            pair_loads(NP - 1)
            for t in range(NT):
                sp.wait_ge(t_out, t + 1)
                sp.dma_start(out[t], xn[:, t, :]).then_inc(stored, 16)
            sp.wait_ge(stored, 16 * NT)

        def column_sums(pe, b):
            pe.wait_ge(t_ctxq, NC * (b + 1))
            if b == 0:
                pe.wait_ge(t_ones, 1)
            for c in range(NC):
                mm = pe.matmul(p_flat[1 + b], ones_b[:], ctx_q[:, b * NC + c, :], start=(c == 0), stop=(c == NC - 1))
            mm.then_inc(t_col, 1)

        def add_column_part(pe, t):
            pe.wait_ge(t_lin, t + 1)
            pe.matmul(acc[t][:], ident[:], corr[:, t // 2, :], start=False, stop=True, skip_group_check=True)

        def transpose_q1(pe, t):
            pe.wait_ge(t_q1, t + 1)
            if t >= 2:
                pe.wait_ge(t_tmp, t - 1)
            for c in range(NC):
                mm = pe.transpose(p_flat[2 + t % 2].bitcast(BF16)[:, c * P:(c + 1) * P],
                                  q1[:, t, c * P:(c + 1) * P], ident_b[:])
            mm.then_inc(t_q1t, 1)

        def quant_product(pe, t):
            pe.wait_ge(t_q1t_out, t + 1)
            for c in range(NC):
                pe.matmul(p_flat[t % 2], q1t[:, t, c, :], ctx_q[:, t // 2 * NC + c, :], start=(c == 0),
                          stop=(c == NC - 1))
            for c in range(NC):
                mm = pe.matmul(p_flat[2 + t % 2][:, 511:512], q1t[:, t, c, :], ones_b[:, 0:1],
                               start=(c == 0), stop=(c == NC - 1))
            mm.then_inc(t_qq, 1)

        def transpose_x3(pe, t):
            pe.wait_ge(t_xn, t + 1)
            for c in range(NC):
                mm = pe.transpose(acc[t][:, c * P:(c + 1) * P], xn[:, t, c * P:(c + 1) * P], ident[:])
            mm.then_inc(t_x3t, 1)

        def low_rank(pe, t):
            pe.wait_ge(t_x3lo, t + 1)
            if t == 0:
                pe.wait_ge(t_lo, 1)
            hi = ra_hi[:].rearrange("p (c n) -> p c n", c=NC)
            lo = ra_lo[:].rearrange("p (c n) -> p c n", c=NC)
            tt = slice(t * P, (t + 1) * P)
            dst = acc[t][:, 0:RA]
            for c in range(NC):
                pe.matmul(dst, xnt_hi[:, c, tt], hi[:, c, :], start=(c == 0), stop=False)
                pe.matmul(dst, xnt_hi[:, c, tt], lo[:, c, :], start=False, stop=False)
                mm = pe.matmul(dst, xnt_lo[:, c, tt], hi[:, c, :], start=False, stop=(c == NC - 1))
            mm.then_inc(t_ra, 1)

        def base_out(pe, t):
            tt = slice(t * P, (t + 1) * P)
            if t == 0:
                pe.wait_ge(w_lo_pool, NS - 1)
                pe.wait_ge(t_tmp, NT)
            for g in range(2):
                hi, lo = pair_parts(g)
                dst = p_flat[t][:, g * PW:(g + 1) * PW]
                for c in range(NC):
                    pe.matmul(dst, xnt_hi[:, c, tt], hi[:, c, :], start=(g == 0 and c == 0), stop=False,
                              skip_group_check=True)
                    pe.matmul(dst, xnt_hi[:, c, tt], lo[:, c, :], start=False, stop=False, skip_group_check=True)
                    pe.matmul(dst, xnt_lo[:, c, tt], hi[:, c, :], start=False, stop=False, skip_group_check=True)

        @block.tensor
        def _(pe):
            pe.wait_ge(consts_made, 1)
            for t in range(NT):
                pe.wait_ge(ln_done, t + 1)
                for c in range(NC):
                    mm = pe.transpose(acc[t][:, c * P:(c + 1) * P], xin[:, t, c * P:(c + 1) * P], ident[:])
                mm.then_inc(xt_ready, 1)

            def project(i, r, before):
                u = before + 4 * i + r
                n = r % 2
                pe.wait_ge(w_lo_dve, u + 1)
                if not (isinstance(u, int) and u < 2):
                    pe.wait_ge(squared, u - 1)
                hi, lo = parts(n)
                for c in range(NC):
                    pe.matmul(acc[n][:], hi[:, c, :], xnt_hi[:, c, :], start=(c == 0), stop=False)
                    pe.matmul(acc[n][:], lo[:, c, :], xnt_hi[:, c, :], start=False, stop=False)
                    if not (isinstance(u, int) and u == 0):
                        mm = pe.matmul(acc[n][:], hi[:, c, :], xnt_lo[:, c, :], start=False,
                                       stop=(c == NC - 1))
                if isinstance(u, int) and u == 0:
                    pe.wait_ge(xt_lo, NT)
                    for c in range(NC):
                        mm = pe.matmul(acc[n][:], hi[:, c, :], xnt_lo[:, c, :], start=False,
                                       stop=(c == NC - 1))
                mm.then_inc(proj_ready, 1)

            def sum_squares(sums, dst, n):
                pe.wait_ge(summed, n)
                for t in range(NT):
                    mm = pe.matmul(dst[:, t:t + 1], sums[:, t * P:(t + 1) * P], ones[:, 0:1],
                                   start=True, stop=True)
                mm.then_inc(ssq_ready, 1)

            pe.wait_ge(xt_hi, NT)
            for r in range(4):
                project(0, r, 0)
            with pe.Fori(1, NH // 4) as i:
                for r in range(4):
                    project(i, r, 0)
            project(0, 0, NH)
            project(0, 1, NH)
            sum_squares(acc_k, p_flat[0], NH)
            project(0, 2, NH)
            pe.wait_ge(diag_made, NT)
            pe.matmul(p_flat[1], ones[:], diag[:].rearrange("p t n -> p (t n)"), start=True, stop=True
                      ).then_inc(rkb_ready, 1)
            project(0, 3, NH)
            with pe.Fori(1, NH // 4) as i:
                for r in range(4):
                    project(i, r, NH)

            def scores(h, b):
                s = 2 * h + b
                if b == 0:
                    pe.wait_ge(kq_lo, 2 * h + 2)
                if not (isinstance(s, int) and s == 0):
                    pe.wait_ge(exp_done, 2 * s)
                kb = slice(b * S, (b + 1) * S)
                for a in range(2):
                    qa = slice(b * S + a * P, b * S + (a + 1) * P)
                    pe.matmul(p_s[:, a, :], q_hi[:, qa], k_hi[:, kb], start=True, stop=False)
                    pe.matmul(p_s[:, a, :], q_lo[:, qa], k_hi[:, kb], start=False, stop=False)
                    mm = pe.matmul(p_s[:, a, :], q_hi[:, qa], k_lo[:, kb], start=False, stop=True)
                mm.then_inc(scores_ready, 1)

            def transpose_probs(s, b):
                pe.wait_ge(p_normed, s + 1)
                for m in range(2):
                    for a in range(2):
                        mm = pe.transpose(p_t[:, m, a * P:(a + 1) * P],
                                          probs[:, b, a, m * P:(m + 1) * P], ident[:])
                mm.then_inc(pt_ready, 1)

            def v_tile(pair, t, par, by, split):
                if t == 0:
                    pe.wait_ge(by, split)
                e = 2 * pair + t // 2
                if t % 2 == 0 and not (isinstance(e, int) and e == 0):
                    pe.wait_ge(v_lo_done, e)
                hi, lo = pair_parts(par)
                tt = slice(t * P, (t + 1) * P)
                for c in range(NC):
                    pe.matmul(p_v[:, t % 2, :], xnt_hi[:, c, tt], hi[:, c, :], start=(c == 0), stop=False)
                    pe.matmul(p_v[:, t % 2, :], xnt_hi[:, c, tt], lo[:, c, :], start=False, stop=False)
                    mm = pe.matmul(p_v[:, t % 2, :], xnt_lo[:, c, tt], hi[:, c, :], start=False,
                                   stop=(c == NC - 1))
                if t % 2:
                    mm.then_inc(v_ready, 1)

            def project_out(h, b, first, last):
                if b == 0 or last:
                    pe.wait_ge(o_lo_done, h + 1 + b)
                    if last:
                        pe.wait_ge(t_lo, 3)
                    else:
                        pe.wait_ge(w_lo_pool, 2 * h + 2)
                oh, ol, wh, wl = (o_last_hi, o_last_lo, wo_last_hi, wo_last_lo) if last else (
                    o_hi, o_lo, wo_hi, wo_lo)
                for t in (2 * b, 2 * b + 1):
                    tt = slice(t * P, (t + 1) * P)
                    pe.matmul(acc[t][:], oh[:, tt], wh[:], start=first, stop=False, skip_group_check=True)
                    pe.matmul(acc[t][:], ol[:, tt], wh[:], start=False, stop=False, skip_group_check=True)
                    mm = pe.matmul(acc[t][:], oh[:, tt], wl[:], start=False, stop=last,
                                   skip_group_check=True)
                    if last:
                        mm.then_inc(t_acc, 1)
                if b == 1 and not last:
                    mm.then_inc(wo_used, 1)

            def probs_v(h, hin, b, par, own_bank=False):
                s = 2 * h + b
                pe.wait_ge(pt_lo_done, s + 1)
                for m in range(2):
                    cols = slice(hin * DH, (hin + 1) * DH)
                    vh, vl = v_hi[:, par, 2 * b + m, cols], v_lo[:, par, 2 * b + m, cols]
                    dst = p_o[:, b * S:(b + 1) * S]
                    if own_bank:
                        dst = p_flat[0][:, b * S:(b + 1) * S]
                    pe.matmul(dst, vh, pt_hi[:, m, :], start=(m == 0), stop=False)
                    pe.matmul(dst, vl, pt_hi[:, m, :], start=False, stop=False)
                    mm = pe.matmul(dst, vh, pt_lo[:, m, :], start=False, stop=(m == 1))
                mm.then_inc(pv_done, 1)

            def pair(p, par, first=False, last=False):
                for j in range(4):
                    b = j % 2
                    h = 2 * p + j // 2
                    s = 2 * h + b
                    if not (last and j == 3):
                        scores(h + b, 1 - b)
                    transpose_probs(s, b)
                    if not last:
                        if first:
                            v_tile(p + 1, j, 1 - par, w_lo_dve, U1 + 4)
                        else:
                            v_tile(p + 1, j, 1 - par, w_lo_pool, 4 * p - 1)
                    if last:
                        for t in ((0, 1), (), (2,), (3,))[j]:
                            pe.wait_ge(xb_done, t + 1)
                            pe.matmul(acc[t][:], ident[:], x_res[:, t, :], start=False, stop=False,
                                      skip_group_check=True)
                    if not (first and j < 2):
                        project_out(h - 1, b, first=(first and j >= 2), last=False)
                    if j == 0:
                        pe.wait_ge(v_lo_done, 2 * p + 2)
                    probs_v(h, j // 2, b, par, own_bank=(last and j == 3))

            v_tile(0, 0, 0, w_lo_dve, U1 + 2)
            v_tile(0, 1, 0, w_lo_dve, U1 + 2)
            sum_squares(acc_q, p_flat[2], U1)
            scores(0, 0)
            v_tile(0, 2, 0, w_lo_dve, U1 + 2)
            v_tile(0, 3, 0, w_lo_dve, U1 + 2)
            pe.wait_ge(ssq_out, 2)
            pair(0, 0, first=True)
            with pe.Fori(0, (NP - 6) // 2) as i:
                pair(2 * i + 1, 1)
                pair(2 * i + 2, 0)
            for p in range(NP - 5, NP - 1):
                pair(p, p % 2)
            pair(NP - 1, 1, last=True)
            project_out(NH - 1, 0, False, True)
            column_sums(pe, 0)
            column_sums(pe, 1)
            project_out(NH - 1, 1, False, True)

            pe.wait_ge(t_corr, 2)
            add_column_part(pe, 0)
            add_column_part(pe, 1)
            transpose_q1(pe, 0)
            transpose_q1(pe, 1)
            quant_product(pe, 0)
            quant_product(pe, 1)
            add_column_part(pe, 2)
            transpose_q1(pe, 2)
            transpose_q1(pe, 3)
            add_column_part(pe, 3)
            quant_product(pe, 2)
            quant_product(pe, 3)
            transpose_x3(pe, 0)
            transpose_x3(pe, 1)
            low_rank(pe, 0)
            base_out(pe, 0)
            transpose_x3(pe, 2)
            low_rank(pe, 1)
            transpose_x3(pe, 3)
            low_rank(pe, 2)
            low_rank(pe, 3)
            base_out(pe, 1)
            base_out(pe, 2)
            pe.wait_ge(t_hw, 1)
            for t in range(NT):
                mm = pe.transpose(acc[0][:, t * P:(t + 1) * P], hw[:, t, :], ident[:])
            mm.then_inc(t_hwt, 1)
            base_out(pe, 3)
            pe.wait_ge(t_lo, 2)
            pe.wait_ge(t_hwlo, 1)
            for t in range(NT):
                y = p_flat[t]
                pe.matmul(y, hwt_hi[:, t, :], bm_hi[:], start=False, stop=False, skip_group_check=True)
                pe.matmul(y, hwt_lo[:, t, :], bm_hi[:], start=False, stop=False, skip_group_check=True)
                pe.matmul(y, hwt_hi[:, t, :], bm_lo[:], start=False, stop=True, skip_group_check=True
                          ).then_inc(t_y, 1)

        @block.scalar
        def _(act):
            def weights_hi(i, r, before, landed):
                u = before + 4 * i + r
                act.wait_ge(w_landed[r], 16 * (landed + i + 1))
                if not (isinstance(u, int) and u < 2):
                    act.wait_ge(proj_ready, u - 1)
                act.copy(w_hi[:, r % 2, 0:NC * DH], raw[:, r, :]).then_inc(w_hi_done, 1)

            def take(i, r, before, dst, bias):
                u = before + 4 * i + r
                act.wait_ge(proj_ready, u + 1)
                if not (isinstance(u, int) and u < 2):
                    act.wait_ge(summed, u - 1)
                h = 4 * i + r
                act.activation(head(dst, h), acc[r % 2][:], ACT.Identity, bias=column(bias, h))
                act.activation(square[:, r % 2, :], acc[r % 2][:], ACT.Square, bias=column(bias, h)
                               ).then_inc(squared, 1)

            for t in range(NT):
                act.wait_ge(xt_ready, t + 1)
                act.copy(xnt_hi[:, :, t * P:(t + 1) * P], acc[t][:].rearrange("p (c n) -> p c n", c=NC)
                         ).then_inc(xt_hi, 1)
                if t == 0:
                    weights_hi(0, 0, 0, 0)
            weights_hi(0, 1, 0, 0)
            act.wait_ge(const_landed, 16 * 5)
            for r in range(2, 4):
                weights_hi(0, r, 0, 0)
                take(0, r - 2, 0, k_all, bk_c)
            with act.Fori(1, NH // 4) as i:
                for r in range(4):
                    weights_hi(i, r, 0, 0)
                    take(i if r >= 2 else i - 1, (r - 2) % 4, 0, k_all, bk_c)
            for r in range(4):
                weights_hi(0, r, NH, NH // 4)
                if r < 2:
                    take(NH // 4 - 1, r + 2, 0, k_all, bk_c)
                else:
                    take(0, r - 2, NH, q_all, bq_c)
            with act.Fori(1, NH // 4) as i:
                for r in range(4):
                    weights_hi(i, r, NH, NH // 4)
                    take(i if r >= 2 else i - 1, (r - 2) % 4, NH, q_all, bq_c)

            def pair_weights_hi(n, buf, half_, landed):
                act.wait_ge(w_landed[n], 16 * (NH // 2 + landed))
                act.copy(w_hi[:, buf, half_ * 512:(half_ + 1) * 512], raw[:, n, :]).then_inc(w_hi_done, 1)

            def split_k_hi(h):
                act.copy(k_hi[:], head(k_all, h)).then_inc(kq_hi, 1)

            def split_q_hi(h):
                act.copy(q_hi[:], head(q_all, h)).then_inc(kq_hi, 1)

            def v_half_hi(pair, e, par):
                act.wait_ge(v_ready, 2 * pair + e + 1)
                act.copy(v_hi[:, par, 2 * e:2 * e + 2, :], p_v[:]).then_inc(v_hi_done, 1)

            def exps(h, b):
                s = 2 * h + b
                act.wait_ge(nb_done, s + 1)
                for a in range(2):
                    act.activation(probs[:, b, a, :], p_s[:, a, :], ACT.Exp, bias=nbias[:, b, a:a + 1],
                                   scale=rq_t[:, 2 * b + a:2 * b + a + 1], accum_out=rsum[:, b, a:a + 1]
                                   ).then_inc(exp_done, 1)

            act.wait_ge(k_normed, 1)
            split_k_hi(0)
            act.wait_ge(squared, NH + 1)
            split_q_hi(0)
            act.wait_ge(proj_ready, U1 - 1)
            pair_weights_hi(0, 0, 0, 1)
            pair_weights_hi(1, 0, 1, 1)
            take(NH // 4 - 1, 2, NH, q_all, bq_c)
            take(NH // 4 - 1, 3, NH, q_all, bq_c)
            pair_weights_hi(0, 1, 0, 2)
            v_half_hi(0, 0, 0)
            pair_weights_hi(1, 1, 1, 2)
            exps(0, 0)
            v_half_hi(0, 1, 0)

            def column_part(b):
                act.wait_ge(t_col, b + 1)
                act.activation(corr[:, b, :], p_flat[1 + b], ACT.Identity, scale=qc[:, 3:4], bias=qc[:, 6:7]
                               ).then_inc(t_corr, 1)

            def last_out_hi(b):
                act.wait_ge(pv_done, NS - 1 + b)
                cols = slice(b * S, (b + 1) * S)
                act.activation(o_last_hi[:, cols], (p_o[:] if b == 0 else p_flat[0])[:, cols], ACT.Identity,
                               bias=bv_c[:, NH - 1:NH]).then_inc(o_hi_done, 1)

            def pair(p, par, last=False):
                for j in range(4):
                    b = j % 2
                    h = 2 * p + j // 2
                    s = 2 * h + b
                    if b == 0 and not (isinstance(h, int) and h == 0):
                        act.wait_ge(pv_done, 2 * h)
                        act.activation(o_hi[:], p_o[:], ACT.Identity, bias=column(bv_c, h - 1)
                                       ).then_inc(o_hi_done, 1)
                    if b == 0 and not (last and j == 2):
                        act.wait_ge(scores_ready, 2 * h + 2)
                        split_k_hi(h + 1)
                        split_q_hi(h + 1)
                    if last and j == 3:
                        last_out_hi(0)
                    act.wait_ge(pt_ready, s + 1)
                    act.copy(pt_hi[:], p_t[:]).then_inc(pt_hi_done, 1)
                    if not (last and j == 3):
                        exps(h + b, 1 - b)
                    if b == 1 and not last:
                        v_half_hi(p + 1, j // 2, 1 - par)
                    if last and j == 0:
                        act.wait_ge(tail_landed[8], 16)
                        act.copy(wo_last_hi[:], wo_last_f[:]).then_inc(t_hi, 1)
                    if last and j == 3:
                        continue
                    if b == 1:
                        act.wait_ge(w_landed[1], 16 * (NH // 2 + 3 + 2 * p + j // 2))
                        if not (isinstance(h, int) and h == 0):
                            act.wait_ge(wo_used, h)
                        act.copy(wo_hi[:], raw[:, 1, :]).then_inc(w_hi_done, 1)
                    else:
                        pair_weights_hi(0, par, j // 2, 3 + 2 * p + j // 2)
                    if isinstance(p, int) and p == NP - 3 and j == 1:
                        act.wait_ge(tail_landed[2], 16)
                        act.copy(ra_hi[:], ra_f[:]).then_inc(t_hi, 1)
                    if isinstance(p, int) and p == NP - 3 and j == 3:
                        act.wait_ge(tail_landed[4], 16)
                        act.copy(bm_hi[:], bm_f[:]).then_inc(t_hi, 1)

            pair(0, 0)
            with act.Fori(0, (NP - 6) // 2) as i:
                pair(2 * i + 1, 1)
                pair(2 * i + 2, 0)
            for p in range(NP - 5, NP - 1):
                pair(p, p % 2)
            pair(NP - 1, 1, last=True)
            last_out_hi(1)

            column_part(0)
            column_part(1)
            def linear(t):
                act.wait_ge(t_coef, t // 2 + 1)
                act.activation(xn[:, t, :], acc[t][:], ACT.Identity, scale=cs[:, t:t + 1], bias=cb[:, t:t + 1]
                               ).then_inc(t_lin, 1)

            def q1_out(t):
                act.wait_ge(t_q1t, t + 1)
                act.copy(q1t[:, t, :, :].rearrange("p c n -> p (c n)"), p_flat[2 + t % 2].bitcast(BF16)[:, 0:D]
                         ).then_inc(t_q1t_out, 1)

            def scaled(t):
                act.wait_ge(t_qq, t + 1)
                act.activation(rsd[:, t:t + 1], p_flat[2 + t % 2][:, 511:512], ACT.Copy, scale=qc[:, 5:6]
                               ).then_inc(t_rsd, 1)
                act.wait_ge(t_rsd, t + 1)
                act.activation(xn[:, t, :], p_flat[t % 2], ACT.Identity, scale=qc[:, 2:3], bias=rsd[:, t:t + 1]
                               ).then_inc(t_tmp, 1)

            def normalise(t):
                act.wait_ge(t_coef, 3 + t)
                act.activation(xn[:, t, :], x_res[:, t, :], ACT.Identity, scale=rstd[:, t:t + 1],
                               bias=cb[:, t:t + 1]).then_inc(t_xn, 1)

            def x3_hi(t):
                act.wait_ge(t_x3t, t + 1)
                act.copy(xnt_hi[:, :, t * P:(t + 1) * P], acc[t][:].rearrange("p (c n) -> p c n", c=NC)
                         ).then_inc(t_x3hi, 1)

            for t in (0, 1):
                linear(t)
            for t in (0, 1):
                q1_out(t)
            for t in (2, 3):
                linear(t)
            for t in (0, 1):
                scaled(t)
            for t in (2, 3):
                q1_out(t)
            normalise(0)
            scaled(2)
            x3_hi(0)
            normalise(1)
            scaled(3)
            x3_hi(1)
            normalise(2)
            normalise(3)
            x3_hi(2)
            x3_hi(3)
            act.wait_ge(t_sub, 1)
            act.activation(pr[:], logit[:], ACT.Exp).then_inc(t_exp, 1)
            act.wait_ge(t_hwt, 1)
            act.copy(hwt_hi[:].rearrange("p t n -> p (t n)"), acc[0][:]).then_inc(t_hwhi, 1)

        @block.gpsimd
        def _(pool):
            made = sem("made")
            pool.memset(ident[:], 0.0).then_inc(made, 1)
            pool.memset(mhalf[:], -0.5).then_inc(made, 1)
            pool.memset(ones[:], 1.0).then_inc(made, 1)
            pool.memset(acc_k[:], 0.0).then_inc(made, 1)
            pool.memset(acc_q[:], 0.0).then_inc(made, 1)
            pool.wait_ge(made, 5)
            pool.affine_select(out=ident[:], in_=ident[:], compare_op=ALU.not_equal, fill=1.0, base=0,
                               pattern=[[-1, P]], channel_multiplier=1).then_inc(consts_made, 1)
            for t in range(NT):
                pool.wait_ge(ln_var, t + 1)
                pool.tensor_tensor(rstd[:, t:t + 1], vare[:, t:t + 1], mhalf[:, t:t + 1], ALU.pow
                                   ).then_inc(gpow, 1)
            pool.wait_ge(consts_made, 1)
            pool.tensor_copy(ident_b[:], ident[:]).then_inc(consts_made, 1)

            def add_square(i, r, before, sums):
                u = before + 4 * i + r
                pool.wait_ge(squared, u + 1)
                if not (isinstance(u, int) and u == 0):
                    pool.wait_ge(summed, u)
                pool.tensor_tensor(sums[:], sums[:], square[:, r % 2, :], ALU.add).then_inc(summed, 1)

            for r in range(4):
                add_square(0, r, 0, acc_k)
            with pool.Fori(1, NH // 4) as i:
                for r in range(4):
                    add_square(i, r, 0, acc_k)
            pool.wait_ge(ssq_out, 1)
            pool.tensor_tensor(rk_t[:], ssq[:], mhalf[:], ALU.pow).then_inc(rms_pow, 1)
            for r in range(4):
                add_square(0, r, NH, acc_q)
            with pool.Fori(1, NH // 4) as i:
                for r in range(4):
                    add_square(i, r, NH, acc_q)

            def chunk_lo(dst, hi, slot, n):
                pool.wait_ge(w_hi_done, U1 + n + 1)
                pool.tensor_tensor(dst, raw[:, slot, :], hi, ALU.subtract).then_inc(w_lo_pool, 1)

            def pair_chunk_lo(buf, half_, slot, n):
                cols = slice(half_ * 512, (half_ + 1) * 512)
                chunk_lo(w_lo[:, buf, cols], w_hi[:, buf, cols], slot, n)

            def split_kq_lo(h):
                pool.wait_ge(kq_hi, 2 * h + 1)
                pool.tensor_tensor(k_lo[:], head(k_all, h), k_hi[:], ALU.subtract).then_inc(kq_lo, 1)
                pool.wait_ge(kq_hi, 2 * h + 2)
                pool.tensor_tensor(q_lo[:], head(q_all, h), q_hi[:], ALU.subtract).then_inc(kq_lo, 1)

            pool.wait_ge(ssq_out, 2)
            pool.tensor_tensor(rq_t[:], ssq[:], mhalf[:], ALU.pow).then_inc(rms_pow, 1)

            def prepare(n):
                if n < NT:
                    pool.wait_ge(tail_landed[3], 16 * (NT + 1))
                    pool.tensor_tensor(x_res[:, n, :], x_res[:, n, :], bo_b[:], ALU.add).then_inc(xb_done, 1)
                elif n == NT:
                    pool.memset(ones_b[:], 1.0).then_inc(t_ones, 1)
                    pool.wait_ge(tail_landed[7], 16)
                    pool.tensor_copy(emf[:], em_i[:]).then_inc(made, 1)
                elif n == NT + 1:
                    pool.wait_ge(made, 6)
                    for e in range(NE):
                        ins = pool.tensor_scalar(onehot[:, e, :], emf[:], float(e), None, ALU.is_equal)
                    ins.then_inc(t_onehot, 1)
                elif n == NT + 2:
                    pool.wait_ge(t_hi, 1)
                    pool.tensor_tensor(ra_lo[:], ra_f[:], ra_hi[:], ALU.subtract).then_inc(t_lo, 1)
                else:
                    pool.wait_ge(t_hi, 2)
                    pool.tensor_tensor(bm_lo[:], bm_f[:], bm_hi[:], ALU.subtract).then_inc(t_lo, 1)

            def pair(p, par, last=False):
                for j in range(4):
                    h = 2 * p + j // 2
                    if j % 2 == 0 and not (last and j == 2):
                        split_kq_lo(h + 1)
                    if last and j == 3:
                        pool.wait_ge(t_hi, 3)
                        pool.tensor_tensor(wo_last_lo[:], wo_last_f[:], wo_last_hi[:], ALU.subtract
                                           ).then_inc(t_lo, 1)
                    elif j % 2:
                        chunk_lo(wo_lo[:], wo_hi[:], 1, 4 + 4 * p + j)
                    else:
                        pair_chunk_lo(par, j // 2, 0, 4 + 4 * p + j)
                    if isinstance(p, int) and NP - 5 <= p < NP - 1 and j % 2 == 0:
                        prepare(2 * (p - (NP - 5)) + j // 2)

            pair(0, 0)
            with pool.Fori(0, (NP - 6) // 2) as i:
                pair(2 * i + 1, 1)
                pair(2 * i + 2, 0)
            for p in range(NP - 5, NP - 1):
                pair(p, p % 2)
            pair(NP - 1, 1, last=True)

            for g in range(2):
                pool.wait_ge(t_var, g + 1)
                pool.tensor_tensor(rstd[:, 2 * g:2 * g + 2], vare[:, 2 * g:2 * g + 2], mhalf[:, 0:2], ALU.pow
                                   ).then_inc(t_pow, 1)
            for t in range(NT):
                pool.wait_ge(t_var, 3 + t)
                pool.tensor_tensor(rstd[:, t:t + 1], vare[:, t:t + 1], mhalf[:, 0:1], ALU.pow).then_inc(t_pow, 1)
            pool.wait_ge(tail_landed[5], 16)
            for t in range(NT):
                pool.wait_ge(t_xn, t + 1)
                pool.tensor_tensor(x_res[:, t, :], x_res[:, t, :], bb_b[:], ALU.add).then_inc(t_xbb, 1)

        @block.vector
        def _(dve):
            links = 0

            def link(ins):
                nonlocal links
                links += 1
                ins.then_inc(chain, 1)
                dve.wait_ge(chain, links)

            def later(ins):
                nonlocal links
                links += 1
                ins.then_inc(chain, 1)
                return links

            def done(n):
                dve.wait_ge(chain, n)

            def x_stats(t):
                dve.wait_ge(x_landed[t], 16)
                return later(dve.bn_stats(stats[:, t, :], xin[:, t, :]))

            def aggregate(t, n):
                done(n)
                return later(dve.bn_aggr(mv[:, t, :], stats[:, t, :]))

            def x_variance(t, n):
                done(n)
                dve.tensor_scalar(vare[:, t:t + 1], mv[:, t, 1:2], EPS_LN, None, ALU.add).then_inc(ln_var, 1)

            def normalise_x(t):
                dve.wait_ge(gpow, t + 1)
                dve.tensor_scalar(xin[:, t, :], xin[:, t, :], mv[:, t, 0:1], rstd[:, t:t + 1],
                                  ALU.subtract, ALU.mult).then_inc(ln_done, 1)

            st0 = x_stats(0)
            st1 = x_stats(1)
            ag0 = aggregate(0, st0)
            st2 = x_stats(2)
            x_variance(0, ag0)
            ag1 = aggregate(1, st1)
            st3 = x_stats(3)
            x_variance(1, ag1)
            ag2 = aggregate(2, st2)
            normalise_x(0)
            x_variance(2, ag2)
            ag3 = aggregate(3, st3)
            normalise_x(1)
            x_variance(3, ag3)
            normalise_x(2)
            normalise_x(3)

            def weights_lo(i, r, before):
                dve.wait_ge(w_hi_done, before + 4 * i + r + 1)
                n = r % 2
                dve.tensor_tensor(w_lo[:, n, 0:NC * DH], raw[:, r, :], w_hi[:, n, 0:NC * DH], ALU.subtract
                                  ).then_inc(w_lo_dve, 1)

            def norm_k(i, r):
                h = 4 * i + r
                dve.scalar_tensor_tensor(out=head(k_all, h), in0=head(k_all, h), scalar=column(g_c, h),
                                         in1=rkb[:], op0=ALU.mult, op1=ALU.mult).then_inc(k_normed, 1)

            for t in range(NT):
                dve.wait_ge(xt_hi, t + 1)
                tt = slice(t * P, (t + 1) * P)
                dve.tensor_tensor(xnt_lo[:, :, tt], acc[t][:].rearrange("p (c n) -> p c n", c=NC),
                                  xnt_hi[:, :, tt], ALU.subtract).then_inc(xt_lo, 1)
                if t == 0:
                    weights_lo(0, 0, 0)
            for r in range(1, 4):
                weights_lo(0, r, 0)
            dve.wait_ge(const_landed, 16 * 5)
            link(dve.scalar_tensor_tensor(out=g_c[:], in0=g_c[:], scalar=float(DH) ** -0.5, in1=gq_c[:],
                                          op0=ALU.mult, op1=ALU.mult))
            with dve.Fori(1, NH // 4) as i:
                for r in range(4):
                    weights_lo(i, r, 0)

            def mean_squares(src, n):
                dve.wait_ge(ssq_ready, n)
                dve.tensor_scalar(ssq[:], src[:, 0:NT], 1.0 / INNER, EPS_RMS, ALU.mult, ALU.add
                                  ).then_inc(ssq_out, 1)

            for r in range(3):
                weights_lo(0, r, NH)
            mean_squares(p_flat[0], 1)
            dve.wait_ge(rms_pow, 1)
            for t in range(NT):
                dve.tensor_scalar(diag[:, t, :], ident[:], rk_t[:, t:t + 1], None, ALU.mult).then_inc(diag_made, 1)
            weights_lo(0, 3, NH)
            dve.wait_ge(rkb_ready, 1)
            link(dve.tensor_copy(rkb[:], p_flat[1]))
            for r in range(4):
                weights_lo(1, r, NH)
                norm_k(0, r)
                norm_k(1, r)
            with dve.Fori(2, NH // 4) as i:
                for r in range(4):
                    weights_lo(i, r, NH)
                    norm_k(i, r)

            def slot_max(h, b):
                s = 2 * h + b
                dve.wait_ge(scores_ready, s + 1)
                dve.tensor_reduce(nmax[:, b, :], p_s[:], AX.X, ALU.max, negate=True).then_inc(max_done, 1)
                dve.wait_ge(max_done, s + 1)
                dve.tensor_tensor(nbias[:, b, :], nmax[:, b, :], rq_t[:, 2 * b:2 * b + 2], ALU.mult
                                  ).then_inc(nb_done, 1)

            def slot_norm(h, b):
                s = 2 * h + b
                dve.wait_ge(exp_done, 2 * s + 2)
                dve.reciprocal(rinv[:, b, :], rsum[:, b, :]).then_inc(rinv_done, 1)
                dve.wait_ge(rinv_done, s + 1)
                dve.tensor_scalar(probs[:, b, 0, :], probs[:, b, 0, :], rinv[:, b, 0:1], None, ALU.mult)
                dve.tensor_scalar(probs[:, b, 1, :], probs[:, b, 1, :], rinv[:, b, 1:2], None, ALU.mult
                                  ).then_inc(p_normed, 1)

            def v_half_lo(pair, e, par):
                dve.wait_ge(v_hi_done, 2 * pair + e + 1)
                dve.tensor_tensor(v_lo[:, par, 2 * e:2 * e + 2, :], p_v[:], v_hi[:, par, 2 * e:2 * e + 2, :],
                                  ALU.subtract).then_inc(v_lo_done, 1)

            def out_lo(h):
                dve.wait_ge(o_hi_done, h + 1)
                dve.scalar_tensor_tensor(out=o_lo[:], in0=p_o[:], scalar=column(bv_c, h), in1=o_hi[:],
                                         op0=ALU.add, op1=ALU.subtract).then_inc(o_lo_done, 1)

            def first_pairs_lo(n):
                dve.wait_ge(w_hi_done, U1 + n + 1)
                cols = slice(n % 2 * 512, n % 2 * 512 + 512)
                dve.tensor_tensor(w_lo[:, n // 2, cols], raw[:, n % 2, :], w_hi[:, n // 2, cols], ALU.subtract
                                  ).then_inc(w_lo_dve, 1)

            dve.wait_ge(kq_hi, 2)
            dve.tensor_tensor(k_lo[:], k_all[:, 0, :], k_hi[:], ALU.subtract).then_inc(kq_lo, 1)
            dve.tensor_tensor(q_lo[:], q_all[:, 0, :], q_hi[:], ALU.subtract).then_inc(kq_lo, 1)
            first_pairs_lo(0)
            first_pairs_lo(1)
            first_pairs_lo(2)
            v_half_lo(0, 0, 0)
            mean_squares(p_flat[2], 2)
            first_pairs_lo(3)
            dve.wait_ge(rms_pow, 2)
            slot_max(0, 0)
            slot_norm(0, 0)
            v_half_lo(0, 1, 0)

            def last_out_lo(b):
                dve.wait_ge(o_hi_done, NH + b)
                cols = slice(b * S, (b + 1) * S)
                dve.scalar_tensor_tensor(out=o_last_lo[:, cols], in0=(p_o[:] if b == 0 else p_flat[0])[:, cols],
                                         scalar=bv_c[:, NH - 1:NH], in1=o_last_hi[:, cols], op0=ALU.add,
                                         op1=ALU.subtract).then_inc(o_lo_done, 1)

            def quantise_ctx(n, step):
                c = ctx_f[:, n, :]
                if step == 0:
                    dve.tensor_scalar(c, c, qc[:, 1:2], qs_b[:, 3:4], ALU.mult, ALU.add).then_inc(quarter, 1)
                elif step == 1:
                    dve.wait_ge(quarter, 2 * n + 1)
                    dve.tensor_scalar(c, c, QMIN, QMAX, ALU.max, ALU.min).then_inc(quarter, 1)
                else:
                    dve.wait_ge(quarter, 2 * n + 2)
                    dve.tensor_scalar(ctx_q[:, n, :], c, ROUND, ROUND + MID, ALU.add, ALU.subtract
                                      ).then_inc(t_ctxq, 1)

            def pair(p, par, last=False, ctx_from=None):
                for j in range(4):
                    b = j % 2
                    h = 2 * p + j // 2
                    s = 2 * h + b
                    end = last and j == 3
                    if b == 0 and not (isinstance(h, int) and h == 0):
                        out_lo(h - 1)
                    if not end:
                        slot_max(h + b, 1 - b)
                    if end:
                        last_out_lo(0)
                    dve.wait_ge(pt_hi_done, s + 1)
                    dve.tensor_tensor(pt_lo[:], p_t[:], pt_hi[:], ALU.subtract).then_inc(pt_lo_done, 1)
                    if not end:
                        slot_norm(h + b, 1 - b)
                    if b == 1 and not last:
                        v_half_lo(p + 1, j // 2, 1 - par)
                    if ctx_from is not None:
                        for step in ((2,) if b else (0, 1)):
                            quantise_ctx(ctx_from + j // 2, step)

            pair(0, 0)
            with dve.Fori(0, (NP - 6) // 2) as i:
                pair(2 * i + 1, 1)
                pair(2 * i + 2, 0)
            dve.wait_ge(tail_landed[0], 16)
            dve.reciprocal(qc[:, 0:1], qs_b[:, 0:1])
            dve.reciprocal(qc[:, 1:2], qs_b[:, 2:3])
            dve.tensor_tensor(qc[:, 2:3], qs_b[:, 0:1], qs_b[:, 2:3], ALU.mult)
            dve.tensor_scalar(qc[:, 3:4], qs_b[:, 1:2], -1.0, MID, ALU.mult, ALU.add)
            link(dve.tensor_scalar(qc[:, 4:5], qs_b[:, 3:4], -1.0, MID, ALU.mult, ALU.add))
            link(dve.tensor_tensor(qc[:, 3:4], qc[:, 3:4], qc[:, 2:3], ALU.mult))
            dve.tensor_tensor(qc[:, 5:6], qc[:, 4:5], qc[:, 2:3], ALU.mult)
            link(dve.scalar_tensor_tensor(out=qc[:, 6:7], in0=qc[:, 4:5], scalar=float(D), in1=qc[:, 3:4],
                                          op0=ALU.mult, op1=ALU.mult))
            dve.wait_ge(tail_landed[1], 32)
            for p in range(NP - 5, NP - 1):
                pair(p, p % 2, ctx_from=2 * (p - (NP - 5)))
            pair(NP - 1, 1, last=True)

            def pair_stats(g):
                for t in (2 * g, 2 * g + 1):
                    dve.wait_ge(t_acc, t + 1)
                    n = later(dve.bn_stats(stats[:, t, :], acc[t][:]))
                return n

            def pair_variance(g, n):
                t0 = 2 * g
                done(n)
                later(dve.bn_aggr(mv[:, t0, :], stats[:, t0, :]))
                done(later(dve.bn_aggr(mv[:, t0 + 1, :], stats[:, t0 + 1, :])))
                dve.tensor_scalar(vare[:, t0:t0 + 2], mv[:, t0:t0 + 2, 1], EPS_LN, None, ALU.add
                                  ).then_inc(t_var, 1)

            def pair_coefficients(g):
                a = slice(2 * g, 2 * g + 2)
                dve.wait_ge(t_pow, g + 1)
                link(dve.tensor_scalar(cs[:, a], rstd[:, a], qc[:, 0:1], None, ALU.mult))
                link(dve.tensor_tensor(cm[:, a], mv[:, a, 0], cs[:, a], ALU.mult))
                dve.tensor_scalar(cb[:, a], cm[:, a], -1.0, qs_b[:, 1:2], ALU.mult, ALU.add).then_inc(t_coef, 1)

            def quantise(t0):
                n = [0, 0]
                for k in range(2):
                    t = t0 + k
                    dve.wait_ge(t_lin, t + 1)
                    n[k] = later(dve.tensor_scalar(xn[:, t, :], xn[:, t, :], QMIN, QMAX, ALU.max, ALU.min))
                    if k == 1:
                        done(n[0])
                        dve.tensor_scalar(q1[:, t0, :], xn[:, t0, :], ROUND, ROUND + MID, ALU.add, ALU.subtract
                                          ).then_inc(t_q1, 1)
                done(n[1])
                dve.tensor_scalar(q1[:, t0 + 1, :], xn[:, t0 + 1, :], ROUND, ROUND + MID, ALU.add, ALU.subtract
                                  ).then_inc(t_q1, 1)

            def second_sum(t):
                dve.wait_ge(t_tmp, t + 1)
                dve.tensor_tensor(x_res[:, t, :], acc[t][:], xn[:, t, :], ALU.add).then_inc(t_x2, 1)

            def stats3(t):
                dve.wait_ge(t_x2, t + 1)
                return later(dve.bn_stats(stats[:, t, :], x_res[:, t, :]))

            def variance3(t, n):
                done(n)
                link(dve.bn_aggr(mv[:, t, :], stats[:, t, :]))
                dve.tensor_scalar(vare[:, t:t + 1], mv[:, t, 1:2], EPS_LN, None, ALU.add).then_inc(t_var, 1)

            def bias3(t):
                dve.wait_ge(t_pow, 3 + t)
                dve.scalar_tensor_tensor(out=cb[:, t:t + 1], in0=mv[:, t, 0:1], scalar=-1.0,
                                         in1=rstd[:, t:t + 1], op0=ALU.mult, op1=ALU.mult).then_inc(t_coef, 1)

            def x3_lo(t):
                dve.wait_ge(t_x3hi, t + 1)
                tt = slice(t * P, (t + 1) * P)
                dve.tensor_tensor(xnt_lo[:, :, tt], acc[t][:].rearrange("p (c n) -> p c n", c=NC),
                                  xnt_hi[:, :, tt], ALU.subtract).then_inc(t_x3lo, 1)

            n = pair_stats(0)
            last_out_lo(1)
            pair_variance(0, n)
            pair_coefficients(0)
            n = pair_stats(1)
            pair_variance(1, n)
            quantise(0)
            pair_coefficients(1)
            quantise(2)
            second_sum(0)
            n0 = stats3(0)
            second_sum(1)
            variance3(0, n0)
            n1 = stats3(1)
            bias3(0)
            variance3(1, n1)
            bias3(1)
            second_sum(2)
            x3_lo(0)
            n2 = stats3(2)
            x3_lo(1)
            variance3(2, n2)
            second_sum(3)
            n3 = stats3(3)
            bias3(2)
            variance3(3, n3)
            bias3(3)
            x3_lo(2)
            x3_lo(3)
            dve.wait_ge(tail_landed[6], 16)
            for t in range(NT):
                dve.wait_ge(t_ra, t + 1)
                n = later(dve.tensor_tensor(logit[:, t, :], acc[t][:, P:P + NR], rb_b[:], ALU.add))
            done(n)

            def wide(a):
                return a.unsqueeze(2).to_broadcast([P, NT, NR])

            link(dve.tensor_reduce(fsm[:, 0:NT], logit[:], AX.X, ALU.max))
            dve.tensor_tensor(logit[:], logit[:], wide(fsm[:, 0:NT]), ALU.subtract).then_inc(t_sub, 1)
            dve.wait_ge(t_exp, 1)
            link(dve.tensor_reduce(fsm[:, NT:2 * NT], pr[:], AX.X, ALU.add))
            link(dve.reciprocal(fsm[:, 2 * NT:3 * NT], fsm[:, NT:2 * NT]))
            link(dve.tensor_tensor(pr[:], pr[:], wide(fsm[:, 2 * NT:3 * NT]), ALU.mult))
            for t in range(NT):
                n = later(dve.max(out=top8[:, t, :], in_=pr[:, t, :]))
            done(n)
            for t in range(NT):
                n = later(dve.match_replace(out=cut[:, t, :], in_to_replace=top8[:, t, :], in_values=pr[:, t, :],
                                            imm_value=-1.0))
            done(n)
            link(dve.scalar_tensor_tensor(out=kept[:], in0=cut[:], scalar=0.0, in1=pr[:],
                                          op0=ALU.is_lt, op1=ALU.mult))
            dve.wait_ge(t_onehot, 1)
            for t in range(NT):
                n = later(dve.tensor_tensor(spread[:, t, :, :], kept[:, t, :].unsqueeze(1).to_broadcast([P, NE, NR]),
                                            onehot[:], ALU.mult))
            done(n)
            link(dve.tensor_reduce(gate[:], spread[:], AX.X, ALU.add))
            for t in range(NT):
                ins = dve.scalar_tensor_tensor(out=hw[:, t, :].rearrange("p (e r) -> p e r", e=NE),
                                               in0=acc[t][:, 0:P].rearrange("p (e r) -> p e r", e=NE), scalar=2.0,
                                               in1=gate[:, t, :].unsqueeze(2).to_broadcast([P, NE, RK]),
                                               op0=ALU.mult, op1=ALU.mult)
            ins.then_inc(t_hw, 1)
            dve.wait_ge(t_hwhi, 1)
            dve.tensor_tensor(hwt_lo[:].rearrange("p t n -> p (t n)"), acc[0][:],
                              hwt_hi[:].rearrange("p t n -> p (t n)"), ALU.subtract).then_inc(t_hwlo, 1)
            for t in range(NT):
                dve.wait_ge(t_xbb, t + 1)
                dve.wait_ge(t_y, t + 1)
                dve.tensor_tensor(xn[:, t, :], p_flat[t], x_res[:, t, :], ALU.add).then_inc(t_out, 1)


def kernel(**inputs):
    import numpy as np
    from concourse import bacc
    from concourse.bass_utils import run_bass_kernel_spmd

    a = {k: np.asarray(v) for k, v in inputs.items()}

    def per_head(w):
        return np.ascontiguousarray(w.reshape(NC, P, NH, DH).transpose(2, 1, 0, 3)).reshape(NH, P, NC * DH)

    def per_pair(w):
        n = w.shape[1] // PW
        t = w.reshape(2, 2, P, n, PW).transpose(3, 0, 2, 1, 4)
        return np.ascontiguousarray(t).reshape(2 * n, P, 2 * PW)

    def columns(v):
        return np.ascontiguousarray(v.reshape(NH, DH).T)

    wv_base = np.concatenate([a["L0_attn_Wv"], a["L0_ffn_base_W"].T], axis=1)
    a_r = np.concatenate([a["L0_ffn_A"].reshape(NE * RK, D), a["L0_ffn_router_W"],
                          np.zeros((1, D), np.float32)], axis=0)
    arrays = {
        "in_x": a["x"].reshape(NT, P, D),
        "in_ctx": np.ascontiguousarray(a["ctx_4096"].reshape(B * NC, P, SKV).transpose(1, 0, 2)),
        "in_wk": per_head(a["L0_attn_Wk"]),
        "in_wq": per_head(a["L0_attn_Wq"]),
        "in_wv": per_pair(wv_base),
        "in_wo": a["L0_attn_Wo"].reshape(NH, DH, D),
        "in_bk": columns(a["L0_attn_bk"]),
        "in_bq": columns(a["L0_attn_bq"]),
        "in_bv": columns(a["L0_attn_bv"]),
        "in_bo": a["L0_attn_bo"],
        "in_gk": columns(a["L0_attn_gk"]),
        "in_gq": columns(a["L0_attn_gq"]),
        "in_qs": np.concatenate([a["L0_xattn_x1_scale"], a["L0_xattn_x1_zp"], a["L0_xattn_x2_scale"],
                                 a["L0_xattn_x2_zp"]]),
        "in_ra": np.ascontiguousarray(a_r.T.reshape(NC, P, RA).transpose(1, 0, 2)).reshape(P, NC * RA),
        "in_bb": a["L0_ffn_base_b"],
        "in_rb": a["L0_ffn_router_b"],
        "in_bm": np.ascontiguousarray(a["L0_ffn_B"].transpose(0, 2, 1)).reshape(NE * RK, D),
        "in_em": a["L0_ffn_expert_map"],
    }
    nc = bacc.Bacc("TRN2", target_bir_lowering=False, num_devices=1)
    args = [nc.dram_tensor(k, v.shape, mybir.dt.from_np(v.dtype), kind="ExternalInput").ap()
            for k, v in arrays.items()]
    y = nc.dram_tensor("out_y", (NT, P, D), F32, kind="ExternalOutput").ap()
    decoder_layer(nc, *args, y)
    r = run_bass_kernel_spmd(nc, [arrays], core_ids=[0])
    return r.results[0]["out_y"].reshape(B, S, D)
```

```python
from contextlib import ExitStack

import concourse.bass as bass
from concourse import mybir

F32 = mybir.dt.float32
F32R = mybir.dt.float32r
BF16 = mybir.dt.bfloat16
I32 = mybir.dt.int32
ALU = mybir.AluOpType
ACT = mybir.ActivationFunctionType
AX = mybir.AxisListType

P = 128
B, S, D = 2, 256, 512
T = B * S
NT = T // P
NC = D // P
SKV = 512
NH, DH = 32, 128
NP = NH // 2
NS = 2 * NH
PW = 2 * DH
INNER = NH * DH
NE, RK, NR = 8, 16, 15
RA = P + NR + 1
EPS_LN, EPS_RMS = 1e-5, 1e-6
ROUND = 12582912.0
WARM_UP = 10
MID = 128.0
QMIN, QMAX = 0.0, 255.0
U1 = 2 * NH


def decoder_layer(nc, x, ctx_t, wk, wq, wv, wo, bk, bq, bv, bo, gk, gq, qscal, ra_w, base_b, router_b, bm_w,
                  expert_map, out):
    st = ExitStack()
    with st:
        def sem(name):
            return st.enter_context(nc.semaphore(name))

        def bank(name, shape, dt=F32):
            return st.enter_context(nc.psum_tensor(name, shape, dt))

        base = (nc.sbuf_base + 63) // 64 * 64
        top = [base]

        def place(name, shape, dt, at=None):
            size = {F32: 4, F32R: 4, BF16: 2, I32: 4}[dt]
            for n in shape[1:]:
                size *= n
            if at is None:
                at = top[0]
                top[0] += (size + 31) // 32 * 32
            return nc.alloc_sbuf_tensor_at(name, shape, dt, offset=at), at

        def here(name, shape, dt, at=None):
            return place(name, shape, dt, at)[0]

        xnt_hi = here("xnt_hi", [P, NC, T], F32R)
        xnt_lo = here("xnt_lo", [P, NC, T], F32R)
        k_all, k_at = place("k_all", [P, NH, T], F32)
        q_all, q_at = place("q_all", [P, NH, T], F32)
        v_hi, vh_at = place("v_hi", [P, 2, NT, PW], F32R)
        v_lo, vl_at = place("v_lo", [P, 2, NT, PW], F32R)
        k_hi = here("k_hi", [P, T], F32R)
        k_lo = here("k_lo", [P, T], F32R)
        q_hi, qh_at = place("q_hi", [P, T], F32R)
        q_lo, ql_at = place("q_lo", [P, T], F32R)
        pt_hi, pt_at = place("pt_hi", [P, 2, S], F32R)
        pt_lo = here("pt_lo", [P, 2, S], F32R)
        o_hi = here("o_hi", [P, T], F32R)
        o_lo = here("o_lo", [P, T], F32R)
        wo_hi = here("wo_hi", [P, D], F32R)
        wo_lo = here("wo_lo", [P, D], F32R)
        raw, raw_at = place("raw", [P, 4, 512], F32)
        probs = here("probs", [P, 2, 2, S], F32, raw_at + 2 * 2048)
        w_hi = here("w_hi", [P, 2, NC * PW], F32R)
        w_lo = here("w_lo", [P, 2, NC * PW], F32R)
        ident = here("ident", [P, P], F32)
        ident_r = here("ident_r", [P, P], F32R)
        ident_b = here("ident_b", [P, P], BF16)
        ones = here("ones", [P, P], F32)
        bk_c = here("bk_c", [P, NH], F32)
        bq_c = here("bq_c", [P, NH], F32)
        bv_c = here("bv_c", [P, NH], F32)
        g_c = here("g_c", [P, NH], F32)
        gq_c = here("gq_c", [P, NH], F32)
        mhalf = here("mhalf", [P, NT], F32)
        ssq = here("ssq", [P, NT], F32)
        rk_t = here("rk_t", [P, NT], F32)
        rq_t = here("rq_t", [P, NT], F32)
        nmax = here("nmax", [P, 2, 2], F32)
        nbias = here("nbias", [P, 2, 2], F32)
        rsum = here("rsum", [P, 2, 2], F32)
        rinv = here("rinv", [P, 2, 2], F32)
        stats = here("stats", [P, NT, 6], F32)
        mv = here("mv", [P, NT, 2], F32)
        vare = here("vare", [P, NT], F32)
        rstd = here("rstd", [P, NT], F32)
        assert top[0] <= nc.sbuf_usable_end, (top[0], nc.sbuf_usable_end)

        half = NT * PW * 4
        acc_k = here("acc_k", [P, T], F32, vh_at + half)
        acc_q = here("acc_q", [P, T], F32, vh_at + half + 2048)
        rkb = here("rkb", [P, T], F32, vl_at + half)
        diag = here("diag", [P, NT, P], F32, vl_at + half + 2048)
        square = here("square", [P, 2, T], F32, pt_at)
        xin = here("xin", [P, NT, D], F32, q_at + (NH - NT) * T * 4)
        KS = T * 4
        x_res = here("x_res", [P, NT, D], F32, k_at)
        xb_lo = here("xb_lo", [P, NT, D], F32R, k_at)
        xb_hi = here("xb_hi", [P, NT, D], F32R, k_at + 22 * KS)
        ctx_f = here("ctx_f", [P, B * NC, SKV], F32, k_at + 4 * KS)
        rb_b = here("rb_b", [P, NR], F32, k_at + 12 * KS)
        em_i = here("em_i", [P, NR], I32, k_at + 12 * KS + 64)
        qs_b = here("qs_b", [P, 4], F32, k_at + 12 * KS + 128)
        bo_b = here("bo_b", [P, D], F32, k_at + 13 * KS)
        bb_b = here("bb_b", [P, D], F32, k_at + 14 * KS)
        bm_f = here("bm_f", [P, D], F32, k_at + 15 * KS)
        ra_f = here("ra_f", [P, NC * RA], F32, k_at + 16 * KS)
        ctx_q = here("ctx_q", [P, B * NC, SKV], BF16, k_at + 18 * KS)
        xn = here("xn", [P, NT, D], F32, q_at)
        q1 = here("q1", [P, NT, D], BF16, q_at + 4 * KS)
        q1t = here("q1t", [P, NT, NC, P], BF16, q_at + 6 * KS)
        corr = here("corr", [P, B, SKV], F32, q_at + 8 * KS)
        hw = here("hw", [P, NT, P], F32, q_at + 10 * KS)
        ones_b = here("ones_b", [P, P], BF16, q_at + 11 * KS)
        small_at = q_at + 12 * KS
        emf = here("emf", [P, NR], F32, small_at)
        onehot = here("onehot", [P, NE, NR], F32, small_at + 128)
        logit = here("logit", [P, NT, NR], F32, small_at + 1024)
        pr = here("pr", [P, NT, NR], F32, small_at + 1536)
        top8 = here("top8", [P, NT, 8], F32, small_at + 2048)
        cut = here("cut", [P, NT, NR], F32, small_at + 2304)
        kept = here("kept", [P, NT, NR], F32, small_at + 2560)
        spread = here("spread", [P, NT, NE, NR], F32, small_at + 3072)
        gate = here("gate", [P, NT, NE], F32, small_at + 5120)
        fsm = here("fsm", [P, 3 * NT], F32, small_at + 5376)
        cs = here("cs", [P, NT], F32, small_at + 5888)
        cm = here("cm", [P, NT], F32, small_at + 5952)
        cb = here("cb", [P, NT], F32, small_at + 6016)
        rsd = here("rsd", [P, NT], F32, small_at + 5632)
        qc = here("qc", [P, 8], F32, small_at + 5760)
        ra_hi = here("ra_hi", [P, NC * RA], F32R, q_at + 16 * KS)
        ra_lo = here("ra_lo", [P, NC * RA], F32R, q_at + 18 * KS)
        bm_hi = here("bm_hi", [P, D], F32R, q_at + 20 * KS)
        bm_lo = here("bm_lo", [P, D], F32R, q_at + 21 * KS)
        wo_last_hi = here("wo_last_hi", [P, D], F32R, q_at + 22 * KS)
        wo_last_lo = here("wo_last_lo", [P, D], F32R, q_at + 23 * KS)
        wo_last_f = here("wo_last_f", [P, D], F32, q_at + 26 * KS)
        o_last_hi = here("o_last_hi", [P, T], F32R, q_at + 24 * KS)
        o_last_lo = here("o_last_lo", [P, T], F32R, q_at + 25 * KS)
        hwt_hi = here("hwt_hi", [P, NT, P], F32R, qh_at)
        hwt_lo = here("hwt_lo", [P, NT, P], F32R, ql_at)

        acc = [bank(f"acc{t}", [P, D]) for t in range(NT)]
        p_v = bank("p_v", [P, 2, PW])
        p_s = bank("p_s", [P, 2, S])
        p_t = bank("p_t", [P, 2, S])
        p_o = bank("p_o", [P, T])
        p_flat = [p_v[:].rearrange("p a b -> p (a b)"), p_s[:].rearrange("p a b -> p (a b)"),
                  p_t[:].rearrange("p a b -> p (a b)"), p_o[:]]

        x_landed = [sem(f"x_landed{t}") for t in range(NT)]
        const_landed = sem("const_landed")
        w_landed = [sem(f"w_landed{r}") for r in range(4)]
        consts_made = sem("consts_made")
        ln_rstd = sem("ln_rstd")
        ln_var = sem("ln_var")
        ln_done = sem("ln_done")
        xt_ready = sem("xt_ready")
        xt_hi = sem("xt_hi")
        xt_lo = sem("xt_lo")
        w_hi_done = sem("w_hi_done")
        w_lo_dve = sem("w_lo_dve")
        w_lo_pool = sem("w_lo_pool")
        proj_ready = sem("proj_ready")
        squared = sem("squared")
        summed = sem("summed")
        ssq_ready = sem("ssq_ready")
        ssq_out = sem("ssq_out")
        rms_done = sem("rms_done")
        diag_made = sem("diag_made")
        rkb_ready = sem("rkb_ready")
        k_normed = sem("k_normed")
        kq_hi = sem("kq_hi")
        kq_lo = sem("kq_lo")
        scores_ready = sem("scores_ready")
        max_done = sem("max_done")
        nb_done = sem("nb_done")
        exp_done = sem("exp_done")
        rinv_done = sem("rinv_done")
        p_normed = sem("p_normed")
        pt_ready = sem("pt_ready")
        pt_hi_done = sem("pt_hi_done")
        pt_lo_done = sem("pt_lo_done")
        pv_done = sem("pv_done")
        o_hi_done = sem("o_hi_done")
        o_lo_done = sem("o_lo_done")
        v_ready = sem("v_ready")
        v_hi_done = sem("v_hi_done")
        v_lo_done = sem("v_lo_done")
        wo_used = sem("wo_used")
        qs_landed = sem("qs_landed")
        ctx_landed = sem("ctx_landed")
        ra_landed = sem("ra_landed")
        x_bo_landed = sem("x_bo_landed")
        bm_landed = sem("bm_landed")
        base_b_landed = sem("base_b_landed")
        router_b_landed = sem("router_b_landed")
        map_landed = sem("map_landed")
        wo_last_landed = sem("wo_last_landed")
        stored = sem("stored")
        ctx_step = sem("ctx_step")
        chain = sem("chain")
        xb_done = sem("xb_done")
        xb_hi_done = sem("xb_hi_done")
        xb_lo_done = sem("xb_lo_done")
        wo_last_hi_done = sem("wo_last_hi_done")
        wo_last_done = sem("wo_last_done")
        x1_ready = sem("x1_ready")
        ones_b_made = sem("ones_b_made")
        ctx_quantised = sem("ctx_quantised")
        col_sums_ready = sem("col_sums_ready")
        col_part_done = sem("col_part_done")
        var_ready = sem("var_ready")
        rstd_ready = sem("rstd_ready")
        coef_ready = sem("coef_ready")
        linear_done = sem("linear_done")
        q1_done = sem("q1_done")
        q1t_ready = sem("q1t_ready")
        q1t_out = sem("q1t_out")
        row_part_done = sem("row_part_done")
        product_ready = sem("product_ready")
        scaled_done = sem("scaled_done")
        x2_done = sem("x2_done")
        x3_normed = sem("x3_normed")
        base_b_added = sem("base_b_added")
        rab_hi_done = sem("rab_hi_done")
        rab_lo_done = sem("rab_lo_done")
        x3t_ready = sem("x3t_ready")
        x3_hi_done = sem("x3_hi_done")
        x3_lo_done = sem("x3_lo_done")
        low_rank_ready = sem("low_rank_ready")
        max_taken = sem("max_taken")
        router_exp_done = sem("router_exp_done")
        experts_marked = sem("experts_marked")
        hw_done = sem("hw_done")
        hwt_ready = sem("hwt_ready")
        hwt_hi_done = sem("hwt_hi_done")
        hwt_lo_done = sem("hwt_lo_done")
        y_ready = sem("y_ready")
        out_done = sem("out_done")

        def peeled(n, first, end):
            return isinstance(n, int) and first <= n < end

        def head(a, h):
            return a[:, bass.ds(h, 1), :].rearrange("p a t -> p (a t)")

        def column(a, h):
            return a[:, bass.ds(h, 1)]

        def parts(n):
            return [w[:, n, 0:NC * DH].rearrange("p (c n) -> p c n", c=NC) for w in (w_hi, w_lo)]

        def pair_parts(n):
            return [w[:, n, :].rearrange("p (c n) -> p c n", c=NC) for w in (w_hi, w_lo)]


        block = st.enter_context(nc.Block())

        @block.sync
        def _(sp):
            for t in range(NT):
                sp.dma_start(xin[:, t, :], x[t]).then_inc(x_landed[t], 16)
            for r in range(4):
                sp.dma_start(raw[:, r, :], wk[r]).then_inc(w_landed[r], 16)
            for dst, src in ((bk_c, bk), (bq_c, bq), (bv_c, bv), (g_c, gk), (gq_c, gq)):
                sp.dma_start(dst[:], src).then_inc(const_landed, 16)

            def load_heads(w, i, before):
                for r in range(4):
                    sp.wait_ge(w_lo_dve, before + 4 * i + r - 3)
                    sp.dma_start(raw[:, r, :], w[bass.ds(4 * i + r, 1)].rearrange("a p n -> (a p) n")
                                 ).then_inc(w_landed[r], 16)

            with sp.Fori(1, NH // 4) as i:
                load_heads(wk, i, 0)
            with sp.Fori(0, NH // 4) as i:
                load_heads(wq, i, NH)

            def load_wv(pair, c, n):
                sp.dma_start(raw[:, n, :], wv[bass.ds(2 * pair + c, 1)].rearrange("a p n -> (a p) n")
                             ).then_inc(w_landed[n], 16)

            def load_wo(h):
                sp.dma_start(raw[:, 1, :], wo[bass.ds(h, 1)].rearrange("a p n -> (a p) n")
                             ).then_inc(w_landed[1], 16)

            for n in range(4):
                sp.wait_ge(w_lo_dve, U1 - 3 + n if n < 2 else U1 + n - 1)
                load_wv(n // 2, n % 2, n % 2)

            def pair_loads(p):
                for j in range(3 if peeled(p, NP - 1, NP) else 4):
                    if peeled(p, 0, 1) and j < 2:
                        sp.wait_ge(w_lo_dve, U1 + 3 + j)
                    else:
                        sp.wait_ge(w_lo_pool, 4 * p + j - 1)
                    if j % 2:
                        load_wo(2 * p + j // 2)
                    else:
                        load_wv(p + 2, j // 2, 0)

            pair_loads(0)
            with sp.Fori(1, 8) as p:
                pair_loads(p)
            sp.wait_ge(scores_ready, 2 * 13)
            sp.dma_start(qs_b[:], qscal.partition_broadcast(P)).then_inc(qs_landed, 16)
            half_ctx = B * NC // 2
            sp.dma_start(ctx_f[:, 0:half_ctx, :], ctx_t[:, 0:half_ctx, :]).then_inc(ctx_landed, 16)
            pair_loads(8)
            sp.dma_start(ctx_f[:, half_ctx:, :], ctx_t[:, half_ctx:, :]).then_inc(ctx_landed, 16)
            pair_loads(9)
            sp.wait_ge(scores_ready, 2 * 18)
            sp.dma_start(bo_b[:], bo.partition_broadcast(P)).then_inc(x_bo_landed, 16)
            for t in range(NT):
                sp.dma_start(x_res[:, t, :], x[t]).then_inc(x_bo_landed, 16)
            pair_loads(10)
            sp.dma_start(ra_f[:], ra_w).then_inc(ra_landed, 16)
            sp.dma_start(bm_f[:], bm_w).then_inc(bm_landed, 16)
            sp.dma_start(bb_b[:], base_b.partition_broadcast(P)).then_inc(base_b_landed, 16)
            sp.dma_start(rb_b[:], router_b.partition_broadcast(P)).then_inc(router_b_landed, 16)
            sp.dma_start(em_i[:], expert_map.partition_broadcast(P)).then_inc(map_landed, 16)
            for p in range(11, NP - 1):
                pair_loads(p)
            sp.dma_start(wo_last_f[:], wo[NH - 1]).then_inc(wo_last_landed, 16)
            pair_loads(NP - 1)
            for t in range(NT):
                sp.wait_ge(out_done, t + 1)
                sp.dma_start(out[t], xn[:, t, :]).then_inc(stored, 16)
            sp.wait_ge(stored, 16 * NT)

        def column_sums(pe, b):
            pe.wait_ge(ctx_quantised, NC * (b + 1))
            if b == 0:
                pe.wait_ge(ones_b_made, 1)
            for c in range(NC):
                mm = pe.matmul(p_flat[1 + b], ones_b[:], ctx_q[:, b * NC + c, :], start=(c == 0), stop=(c == NC - 1))
            mm.then_inc(col_sums_ready, 1)

        def add_column_part(pe, t):
            pe.wait_ge(linear_done, t + 1)
            pe.matmul(acc[t][:], ident[:], corr[:, t // 2, :], start=False, stop=True, skip_group_check=True)

        def transpose_q1(pe, t):
            pe.wait_ge(q1_done, t + 1)
            if t >= 2:
                pe.wait_ge(scaled_done, t - 1)
            for c in range(NC):
                mm = pe.transpose(p_flat[2 + t % 2].bitcast(BF16)[:, c * P:(c + 1) * P],
                                  q1[:, t, c * P:(c + 1) * P], ident_b[:])
            mm.then_inc(q1t_ready, 1)

        def quant_product(pe, t):
            pe.wait_ge(q1t_out, t + 1)
            for c in range(NC):
                pe.matmul(p_flat[t % 2], q1t[:, t, c, :], ctx_q[:, t // 2 * NC + c, :], start=(c == 0),
                          stop=(c == NC - 1))
            for c in range(NC):
                mm = pe.matmul(p_flat[2 + t % 2][:, 511:512], q1t[:, t, c, :], ones_b[:, 0:1],
                               start=(c == 0), stop=(c == NC - 1))
            mm.then_inc(product_ready, 1)

        def transpose_x3(pe, t):
            pe.wait_ge(x3_normed, t + 1)
            for c in range(NC):
                mm = pe.transpose(acc[t][:, c * P:(c + 1) * P], xn[:, t, c * P:(c + 1) * P], ident[:])
            mm.then_inc(x3t_ready, 1)

        def low_rank(pe, t):
            pe.wait_ge(x3_lo_done, t + 1)
            if t == 0:
                pe.wait_ge(rab_lo_done, 1)
            hi = ra_hi[:].rearrange("p (c n) -> p c n", c=NC)
            lo = ra_lo[:].rearrange("p (c n) -> p c n", c=NC)
            tt = slice(t * P, (t + 1) * P)
            dst = acc[t][:, 0:RA]
            for c in range(NC):
                pe.matmul(dst, xnt_hi[:, c, tt], hi[:, c, :], start=(c == 0), stop=False)
                pe.matmul(dst, xnt_hi[:, c, tt], lo[:, c, :], start=False, stop=False)
                mm = pe.matmul(dst, xnt_lo[:, c, tt], hi[:, c, :], start=False, stop=(c == NC - 1))
            mm.then_inc(low_rank_ready, 1)

        def base_out(pe, t):
            tt = slice(t * P, (t + 1) * P)
            if t == 0:
                pe.wait_ge(w_lo_pool, NS - 1)
                pe.wait_ge(scaled_done, NT)
            for g in range(2):
                hi, lo = pair_parts(g)
                dst = p_flat[t][:, g * PW:(g + 1) * PW]
                for c in range(NC):
                    pe.matmul(dst, xnt_hi[:, c, tt], hi[:, c, :], start=(g == 0 and c == 0), stop=False,
                              skip_group_check=True)
                    pe.matmul(dst, xnt_hi[:, c, tt], lo[:, c, :], start=False, stop=False, skip_group_check=True)
                    pe.matmul(dst, xnt_lo[:, c, tt], hi[:, c, :], start=False, stop=False, skip_group_check=True)

        @block.tensor
        def _(pe):
            pe.wait_ge(consts_made, 1)
            for n in range(WARM_UP):
                pe.matmul(acc[0][:, 0:P], ident[:], ones[:], start=True, stop=True)
            for t in range(NT):
                pe.wait_ge(ln_done, t + 1)
                for c in range(NC):
                    mm = pe.transpose(p_flat[t][:, c * P:(c + 1) * P], xin[:, t, c * P:(c + 1) * P], ident[:])
                mm.then_inc(xt_ready, 1)

            def project(i, r, before):
                u = before + 4 * i + r
                n = r % 2
                pe.wait_ge(w_lo_dve, u + 1)
                if not peeled(u, 0, 2):
                    pe.wait_ge(squared, u - 1)
                hi, lo = parts(n)
                for c in range(NC):
                    pe.matmul(acc[n][:], hi[:, c, :], xnt_hi[:, c, :], start=(c == 0), stop=False)
                    pe.matmul(acc[n][:], lo[:, c, :], xnt_hi[:, c, :], start=False, stop=False)
                    if not peeled(u, 0, 1):
                        mm = pe.matmul(acc[n][:], hi[:, c, :], xnt_lo[:, c, :], start=False,
                                       stop=(c == NC - 1))
                if peeled(u, 0, 1):
                    pe.wait_ge(xt_lo, NT)
                    for c in range(NC):
                        mm = pe.matmul(acc[n][:], hi[:, c, :], xnt_lo[:, c, :], start=False,
                                       stop=(c == NC - 1))
                mm.then_inc(proj_ready, 1)

            def sum_squares(sums, dst, n):
                pe.wait_ge(summed, n)
                for t in range(NT):
                    mm = pe.matmul(dst[:, t:t + 1], sums[:, t * P:(t + 1) * P], ones[:, 0:1],
                                   start=True, stop=True)
                mm.then_inc(ssq_ready, 1)

            pe.wait_ge(xt_hi, NT)
            for r in range(4):
                project(0, r, 0)
            with pe.Fori(1, NH // 4) as i:
                for r in range(4):
                    project(i, r, 0)
            project(0, 0, NH)
            project(0, 1, NH)
            sum_squares(acc_k, p_flat[0], NH)
            project(0, 2, NH)
            pe.wait_ge(diag_made, NT)
            pe.matmul(p_flat[1], ones[:], diag[:].rearrange("p t n -> p (t n)"), start=True, stop=True
                      ).then_inc(rkb_ready, 1)
            project(0, 3, NH)
            with pe.Fori(1, NH // 4) as i:
                for r in range(4):
                    project(i, r, NH)

            def scores(h, b):
                s = 2 * h + b
                if b == 0:
                    pe.wait_ge(kq_lo, 2 * h + 2)
                if not peeled(s, 0, 1):
                    pe.wait_ge(exp_done, 2 * s)
                kb = slice(b * S, (b + 1) * S)
                for a in range(2):
                    qa = slice(b * S + a * P, b * S + (a + 1) * P)
                    pe.matmul(p_s[:, a, :], q_hi[:, qa], k_hi[:, kb], start=True, stop=False)
                    pe.matmul(p_s[:, a, :], q_lo[:, qa], k_hi[:, kb], start=False, stop=False)
                    mm = pe.matmul(p_s[:, a, :], q_hi[:, qa], k_lo[:, kb], start=False, stop=True)
                mm.then_inc(scores_ready, 1)

            def transpose_probs(s, b):
                pe.wait_ge(p_normed, s + 1)
                for m in range(2):
                    for a in range(2):
                        mm = pe.transpose(p_t[:, m, a * P:(a + 1) * P],
                                          probs[:, b, a, m * P:(m + 1) * P], ident[:])
                mm.then_inc(pt_ready, 1)

            def v_tile(pair, t, par, by, split):
                if t == 0:
                    pe.wait_ge(by, split)
                e = 2 * pair + t // 2
                if t % 2 == 0 and not peeled(e, 0, 1):
                    pe.wait_ge(v_lo_done, e)
                hi, lo = pair_parts(par)
                tt = slice(t * P, (t + 1) * P)
                for c in range(NC):
                    pe.matmul(p_v[:, t % 2, :], xnt_hi[:, c, tt], hi[:, c, :], start=(c == 0), stop=False)
                    pe.matmul(p_v[:, t % 2, :], xnt_hi[:, c, tt], lo[:, c, :], start=False, stop=False)
                    mm = pe.matmul(p_v[:, t % 2, :], xnt_lo[:, c, tt], hi[:, c, :], start=False,
                                   stop=(c == NC - 1))
                if t % 2:
                    mm.then_inc(v_ready, 1)

            def project_out(h, b, first, last):
                if b == 0 or last:
                    pe.wait_ge(o_lo_done, h + 1 + b)
                    if last:
                        pe.wait_ge(wo_last_done, 1)
                    else:
                        pe.wait_ge(w_lo_pool, 2 * h + 2)
                oh, ol, wh, wl = (o_last_hi, o_last_lo, wo_last_hi, wo_last_lo) if last else (
                    o_hi, o_lo, wo_hi, wo_lo)
                for t in (2 * b, 2 * b + 1):
                    tt = slice(t * P, (t + 1) * P)
                    pe.matmul(acc[t][:], oh[:, tt], wh[:], start=first, stop=False, skip_group_check=True)
                    pe.matmul(acc[t][:], ol[:, tt], wh[:], start=False, stop=False, skip_group_check=True)
                    mm = pe.matmul(acc[t][:], oh[:, tt], wl[:], start=False, stop=last,
                                   skip_group_check=True)
                    if last:
                        mm.then_inc(x1_ready, 1)
                if b == 1 and not last:
                    mm.then_inc(wo_used, 1)

            def probs_v(h, within, b, par, own_bank=False):
                s = 2 * h + b
                pe.wait_ge(pt_lo_done, s + 1)
                for m in range(2):
                    cols = slice(within * DH, (within + 1) * DH)
                    vh, vl = v_hi[:, par, 2 * b + m, cols], v_lo[:, par, 2 * b + m, cols]
                    dst = p_o[:, b * S:(b + 1) * S]
                    if own_bank:
                        dst = p_flat[0][:, b * S:(b + 1) * S]
                    pe.matmul(dst, vh, pt_hi[:, m, :], start=(m == 0), stop=False)
                    pe.matmul(dst, vl, pt_hi[:, m, :], start=False, stop=False)
                    mm = pe.matmul(dst, vh, pt_lo[:, m, :], start=False, stop=(m == 1))
                mm.then_inc(pv_done, 1)

            def pair(p, par, first=False, last=False):
                for j in range(4):
                    b = j % 2
                    h = 2 * p + j // 2
                    s = 2 * h + b
                    if not (last and j == 3):
                        scores(h + b, 1 - b)
                    transpose_probs(s, b)
                    if not last:
                        if first:
                            v_tile(p + 1, j, 1 - par, w_lo_dve, U1 + 4)
                        else:
                            v_tile(p + 1, j, 1 - par, w_lo_pool, 4 * p - 1)
                    if last:
                        for t in ((0, 1), (), (2,), (3,))[j]:
                            pe.wait_ge(xb_lo_done, t + 1)
                            for part in (xb_hi, xb_lo):
                                pe.matmul(acc[t][:], ident_r[:], part[:, t, :], start=False, stop=False,
                                          skip_group_check=True)
                    if not (first and j < 2):
                        project_out(h - 1, b, first=(first and j >= 2), last=False)
                    if j == 0:
                        pe.wait_ge(v_lo_done, 2 * p + 2)
                    probs_v(h, j // 2, b, par, own_bank=(last and j == 3))

            v_tile(0, 0, 0, w_lo_dve, U1 + 2)
            v_tile(0, 1, 0, w_lo_dve, U1 + 2)
            sum_squares(acc_q, p_flat[2], U1)
            scores(0, 0)
            v_tile(0, 2, 0, w_lo_dve, U1 + 2)
            v_tile(0, 3, 0, w_lo_dve, U1 + 2)
            pe.wait_ge(ssq_out, 2)
            pair(0, 0, first=True)
            with pe.Fori(0, (NP - 6) // 2) as i:
                pair(2 * i + 1, 1)
                pair(2 * i + 2, 0)
            for p in range(NP - 5, NP - 1):
                pair(p, p % 2)
            pair(NP - 1, 1, last=True)
            project_out(NH - 1, 0, False, True)
            column_sums(pe, 0)
            column_sums(pe, 1)
            project_out(NH - 1, 1, False, True)

            pe.wait_ge(col_part_done, 2)
            add_column_part(pe, 0)
            add_column_part(pe, 1)
            transpose_q1(pe, 0)
            transpose_q1(pe, 1)
            quant_product(pe, 0)
            quant_product(pe, 1)
            add_column_part(pe, 2)
            transpose_q1(pe, 2)
            transpose_q1(pe, 3)
            add_column_part(pe, 3)
            quant_product(pe, 2)
            quant_product(pe, 3)
            transpose_x3(pe, 0)
            transpose_x3(pe, 1)
            low_rank(pe, 0)
            base_out(pe, 0)
            transpose_x3(pe, 2)
            low_rank(pe, 1)
            transpose_x3(pe, 3)
            low_rank(pe, 2)
            low_rank(pe, 3)
            base_out(pe, 1)
            base_out(pe, 2)
            pe.wait_ge(hw_done, 1)
            for t in range(NT):
                mm = pe.transpose(acc[0][:, t * P:(t + 1) * P], hw[:, t, :], ident[:])
            mm.then_inc(hwt_ready, 1)
            base_out(pe, 3)
            pe.wait_ge(rab_lo_done, 2)
            pe.wait_ge(hwt_lo_done, 1)
            for t in range(NT):
                y = p_flat[t]
                pe.matmul(y, hwt_hi[:, t, :], bm_hi[:], start=False, stop=False, skip_group_check=True)
                pe.matmul(y, hwt_lo[:, t, :], bm_hi[:], start=False, stop=False, skip_group_check=True)
                pe.matmul(y, hwt_hi[:, t, :], bm_lo[:], start=False, stop=True, skip_group_check=True
                          ).then_inc(y_ready, 1)

        @block.scalar
        def _(act):
            def weights_hi(i, r, before, landed):
                u = before + 4 * i + r
                act.wait_ge(w_landed[r], 16 * (landed + i + 1))
                if not peeled(u, 0, 2):
                    act.wait_ge(proj_ready, u - 1)
                act.copy(w_hi[:, r % 2, 0:NC * DH], raw[:, r, :]).then_inc(w_hi_done, 1)

            def take(i, r, before, dst, bias):
                u = before + 4 * i + r
                act.wait_ge(proj_ready, u + 1)
                if not peeled(u, 0, 2):
                    act.wait_ge(summed, u - 1)
                h = 4 * i + r
                if peeled(u, U1 - 1, U1):
                    act.activation(square[:, r % 2, :], acc[r % 2][:], ACT.Square, bias=column(bias, h)
                                   ).then_inc(squared, 1)
                    act.activation(head(dst, h), acc[r % 2][:], ACT.Identity, bias=column(bias, h))
                else:
                    act.activation(head(dst, h), acc[r % 2][:], ACT.Identity, bias=column(bias, h))
                    act.activation(square[:, r % 2, :], acc[r % 2][:], ACT.Square, bias=column(bias, h)
                                   ).then_inc(squared, 1)

            act.wait_ge(consts_made, 1)
            act.copy(ident_r[:], ident[:])
            weights_hi(0, 0, 0, 0)
            for t in range(NT):
                act.wait_ge(xt_ready, t + 1)
                act.copy(xnt_hi[:, :, t * P:(t + 1) * P], p_flat[t].rearrange("p (c n) -> p c n", c=NC)
                         ).then_inc(xt_hi, 1)
            weights_hi(0, 1, 0, 0)
            act.wait_ge(const_landed, 16 * 5)
            for r in range(2, 4):
                weights_hi(0, r, 0, 0)
                take(0, r - 2, 0, k_all, bk_c)
            with act.Fori(1, NH // 4) as i:
                for r in range(4):
                    weights_hi(i, r, 0, 0)
                    take(i if r >= 2 else i - 1, (r - 2) % 4, 0, k_all, bk_c)
            for r in range(4):
                weights_hi(0, r, NH, NH // 4)
                if r < 2:
                    take(NH // 4 - 1, r + 2, 0, k_all, bk_c)
                else:
                    take(0, r - 2, NH, q_all, bq_c)
            with act.Fori(1, NH // 4) as i:
                for r in range(4):
                    weights_hi(i, r, NH, NH // 4)
                    take(i if r >= 2 else i - 1, (r - 2) % 4, NH, q_all, bq_c)

            def pair_weights_hi(n, buf, half_, landed):
                act.wait_ge(w_landed[n], 16 * (NH // 2 + landed))
                act.copy(w_hi[:, buf, half_ * 512:(half_ + 1) * 512], raw[:, n, :]).then_inc(w_hi_done, 1)

            def split_k_hi(h):
                act.copy(k_hi[:], head(k_all, h)).then_inc(kq_hi, 1)

            def split_q_hi(h):
                act.copy(q_hi[:], head(q_all, h)).then_inc(kq_hi, 1)

            def v_half_hi(pair, e, par):
                act.wait_ge(v_ready, 2 * pair + e + 1)
                act.copy(v_hi[:, par, 2 * e:2 * e + 2, :], p_v[:]).then_inc(v_hi_done, 1)

            def exps(h, b):
                s = 2 * h + b
                act.wait_ge(nb_done, s + 1)
                for a in range(2):
                    act.activation(probs[:, b, a, :], p_s[:, a, :], ACT.Exp, bias=nbias[:, b, a:a + 1],
                                   scale=rq_t[:, 2 * b + a:2 * b + a + 1], accum_out=rsum[:, b, a:a + 1]
                                   ).then_inc(exp_done, 1)

            act.wait_ge(k_normed, 1)
            split_k_hi(0)
            act.wait_ge(squared, NH + 1)
            split_q_hi(0)
            act.wait_ge(proj_ready, U1 - 1)
            pair_weights_hi(0, 0, 0, 1)
            pair_weights_hi(1, 0, 1, 1)
            take(NH // 4 - 1, 2, NH, q_all, bq_c)
            take(NH // 4 - 1, 3, NH, q_all, bq_c)
            pair_weights_hi(0, 1, 0, 2)
            v_half_hi(0, 0, 0)
            pair_weights_hi(1, 1, 1, 2)
            exps(0, 0)
            v_half_hi(0, 1, 0)

            def column_part(b):
                act.wait_ge(col_sums_ready, b + 1)
                act.activation(corr[:, b, :], p_flat[1 + b], ACT.Identity, scale=qc[:, 3:4], bias=qc[:, 6:7]
                               ).then_inc(col_part_done, 1)

            def last_out_hi(b):
                act.wait_ge(pv_done, NS - 1 + b)
                cols = slice(b * S, (b + 1) * S)
                act.activation(o_last_hi[:, cols], (p_o[:] if b == 0 else p_flat[0])[:, cols], ACT.Identity,
                               bias=bv_c[:, NH - 1:NH]).then_inc(o_hi_done, 1)

            def pair(p, par, last=False):
                for j in range(4):
                    b = j % 2
                    h = 2 * p + j // 2
                    s = 2 * h + b
                    if b == 0 and not peeled(h, 0, 1):
                        act.wait_ge(pv_done, 2 * h)
                        act.activation(o_hi[:], p_o[:], ACT.Identity, bias=column(bv_c, h - 1)
                                       ).then_inc(o_hi_done, 1)
                    if b == 0 and not (last and j == 2):
                        act.wait_ge(scores_ready, 2 * h + 2)
                        split_k_hi(h + 1)
                        if not peeled(s, 0, 1):
                            split_q_hi(h + 1)
                    if last and j == 3:
                        last_out_hi(0)
                    act.wait_ge(pt_ready, s + 1)
                    act.copy(pt_hi[:], p_t[:]).then_inc(pt_hi_done, 1)
                    if peeled(s, 0, 1):
                        split_q_hi(1)
                    if not (last and j == 3):
                        exps(h + b, 1 - b)
                    if b == 1 and not last:
                        v_half_hi(p + 1, j // 2, 1 - par)
                    if last and j == 0:
                        act.wait_ge(wo_last_landed, 16)
                        act.copy(wo_last_hi[:], wo_last_f[:]).then_inc(wo_last_hi_done, 1)
                    if last and j == 3:
                        pass
                    elif b == 1:
                        act.wait_ge(w_landed[1], 16 * (NH // 2 + 3 + 2 * p + j // 2))
                        if not peeled(h, 0, 1):
                            act.wait_ge(wo_used, h)
                        act.copy(wo_hi[:], raw[:, 1, :]).then_inc(w_hi_done, 1)
                    else:
                        pair_weights_hi(0, par, j // 2, 3 + 2 * p + j // 2)
                    if peeled(p, NP - 3, NP - 1) and b == 0:
                        t = 2 * (p - (NP - 3)) + j // 2
                        act.wait_ge(xb_done, t + 1)
                        act.copy(xb_hi[:, t, :], x_res[:, t, :]).then_inc(xb_hi_done, 1)

            pair(0, 0)
            with act.Fori(0, (NP - 6) // 2) as i:
                pair(2 * i + 1, 1)
                pair(2 * i + 2, 0)
            for p in range(NP - 5, NP - 1):
                pair(p, p % 2)
            pair(NP - 1, 1, last=True)
            act.wait_ge(ra_landed, 16)
            act.copy(ra_hi[:], ra_f[:]).then_inc(rab_hi_done, 1)
            act.wait_ge(bm_landed, 16)
            act.copy(bm_hi[:], bm_f[:]).then_inc(rab_hi_done, 1)
            last_out_hi(1)

            column_part(0)
            column_part(1)

            def linear(t):
                act.wait_ge(coef_ready, t // 2 + 1)
                act.activation(xn[:, t, :], acc[t][:], ACT.Identity, scale=cs[:, t:t + 1], bias=cb[:, t:t + 1]
                               ).then_inc(linear_done, 1)

            def q1_out(t):
                act.wait_ge(q1t_ready, t + 1)
                act.copy(q1t[:, t, :, :].rearrange("p c n -> p (c n)"), p_flat[2 + t % 2].bitcast(BF16)[:, 0:D]
                         ).then_inc(q1t_out, 1)

            def scaled(t):
                act.wait_ge(product_ready, t + 1)
                act.activation(rsd[:, t:t + 1], p_flat[2 + t % 2][:, 511:512], ACT.Copy, scale=qc[:, 5:6]
                               ).then_inc(row_part_done, 1)
                act.wait_ge(row_part_done, t + 1)
                act.activation(xn[:, t, :], p_flat[t % 2], ACT.Identity, scale=qc[:, 2:3], bias=rsd[:, t:t + 1]
                               ).then_inc(scaled_done, 1)

            def normalise(t):
                act.wait_ge(coef_ready, 3 + t)
                act.activation(xn[:, t, :], x_res[:, t, :], ACT.Identity, scale=rstd[:, t:t + 1],
                               bias=cb[:, t:t + 1]).then_inc(x3_normed, 1)

            def x3_hi(t):
                act.wait_ge(x3t_ready, t + 1)
                act.copy(xnt_hi[:, :, t * P:(t + 1) * P], acc[t][:].rearrange("p (c n) -> p c n", c=NC)
                         ).then_inc(x3_hi_done, 1)

            for t in (0, 1):
                linear(t)
            for t in (0, 1):
                q1_out(t)
            for t in (2, 3):
                linear(t)
            for t in (0, 1):
                scaled(t)
            for t in (2, 3):
                q1_out(t)
            normalise(0)
            scaled(2)
            x3_hi(0)
            normalise(1)
            scaled(3)
            x3_hi(1)
            normalise(2)
            normalise(3)
            x3_hi(2)
            x3_hi(3)
            act.wait_ge(max_taken, 1)
            act.activation(pr[:], logit[:], ACT.Exp).then_inc(router_exp_done, 1)
            act.wait_ge(hwt_ready, 1)
            act.copy(hwt_hi[:].rearrange("p t n -> p (t n)"), acc[0][:]).then_inc(hwt_hi_done, 1)

        @block.gpsimd
        def _(pool):
            made = sem("made")
            pool.memset(ident[:], 0.0).then_inc(made, 1)
            pool.memset(mhalf[:], -0.5).then_inc(made, 1)
            pool.memset(ones[:], 1.0).then_inc(made, 1)
            pool.memset(acc_k[:], 0.0).then_inc(made, 1)
            pool.memset(acc_q[:], 0.0).then_inc(made, 1)
            pool.wait_ge(made, 5)
            pool.affine_select(out=ident[:], in_=ident[:], compare_op=ALU.not_equal, fill=1.0, base=0,
                               pattern=[[-1, P]], channel_multiplier=1).then_inc(consts_made, 1)
            for t in range(NT):
                pool.wait_ge(ln_var, t + 1)
                pool.tensor_tensor(rstd[:, t:t + 1], vare[:, t:t + 1], mhalf[:, t:t + 1], ALU.pow
                                   ).then_inc(ln_rstd, 1)
            pool.wait_ge(consts_made, 1)
            pool.tensor_copy(ident_b[:], ident[:]).then_inc(consts_made, 1)

            def add_square(i, r, before, sums):
                u = before + 4 * i + r
                pool.wait_ge(squared, u + 1)
                if not peeled(u, 0, 1):
                    pool.wait_ge(summed, u)
                pool.tensor_tensor(sums[:], sums[:], square[:, r % 2, :], ALU.add).then_inc(summed, 1)

            for r in range(4):
                add_square(0, r, 0, acc_k)
            with pool.Fori(1, NH // 4) as i:
                for r in range(4):
                    add_square(i, r, 0, acc_k)
            pool.wait_ge(ssq_out, 1)
            pool.tensor_tensor(rk_t[:], ssq[:], mhalf[:], ALU.pow).then_inc(rms_done, 1)
            for r in range(4):
                add_square(0, r, NH, acc_q)
            with pool.Fori(1, NH // 4) as i:
                for r in range(4):
                    add_square(i, r, NH, acc_q)

            def chunk_lo(dst, hi, slot, n):
                pool.wait_ge(w_hi_done, U1 + n + 1)
                pool.tensor_tensor(dst, raw[:, slot, :], hi, ALU.subtract).then_inc(w_lo_pool, 1)

            def pair_chunk_lo(buf, half_, slot, n):
                cols = slice(half_ * 512, (half_ + 1) * 512)
                chunk_lo(w_lo[:, buf, cols], w_hi[:, buf, cols], slot, n)

            def split_kq_lo(h):
                pool.wait_ge(kq_hi, 2 * h + 1)
                pool.tensor_tensor(k_lo[:], head(k_all, h), k_hi[:], ALU.subtract).then_inc(kq_lo, 1)
                pool.wait_ge(kq_hi, 2 * h + 2)
                pool.tensor_tensor(q_lo[:], head(q_all, h), q_hi[:], ALU.subtract).then_inc(kq_lo, 1)

            pool.wait_ge(ssq_out, 2)
            pool.tensor_tensor(rq_t[:], ssq[:], mhalf[:], ALU.pow).then_inc(rms_done, 1)

            def mark_experts():
                pool.wait_ge(map_landed, 16)
                pool.tensor_copy(emf[:], em_i[:]).then_inc(made, 1)
                pool.wait_ge(made, 6)
                for e in range(NE):
                    ins = pool.tensor_scalar(onehot[:, e, :], emf[:], float(e), None, ALU.is_equal)
                ins.then_inc(experts_marked, 1)

            def prepare(n):
                if n == 0:
                    pool.memset(ones_b[:], 1.0).then_inc(ones_b_made, 1)
                if n < NT:
                    pool.wait_ge(x_bo_landed, 16 * (NT + 1))
                    pool.tensor_tensor(x_res[:, n, :], x_res[:, n, :], bo_b[:], ALU.add).then_inc(xb_done, 1)
                else:
                    t = n - NT
                    pool.wait_ge(xb_hi_done, t + 1)
                    pool.tensor_tensor(xb_lo[:, t, :], x_res[:, t, :], xb_hi[:, t, :], ALU.subtract
                                       ).then_inc(xb_lo_done, 1)

            def split_low_rank():
                pool.wait_ge(rab_hi_done, 1)
                pool.tensor_tensor(ra_lo[:], ra_f[:], ra_hi[:], ALU.subtract).then_inc(rab_lo_done, 1)
                pool.wait_ge(rab_hi_done, 2)
                pool.tensor_tensor(bm_lo[:], bm_f[:], bm_hi[:], ALU.subtract).then_inc(rab_lo_done, 1)

            def pair(p, par, last=False):
                for j in range(4):
                    h = 2 * p + j // 2
                    if j % 2 == 0 and not (last and j == 2):
                        split_kq_lo(h + 1)
                    if last and j == 3:
                        split_low_rank()
                        break
                    if last and j == 2:
                        pool.wait_ge(wo_last_hi_done, 1)
                        pool.tensor_tensor(wo_last_lo[:], wo_last_f[:], wo_last_hi[:], ALU.subtract
                                           ).then_inc(wo_last_done, 1)
                    if j % 2:
                        chunk_lo(wo_lo[:], wo_hi[:], 1, 4 + 4 * p + j)
                    else:
                        pair_chunk_lo(par, j // 2, 0, 4 + 4 * p + j)
                    if peeled(p, NP - 5, NP - 1) and j % 2 == 0:
                        prepare(2 * (p - (NP - 5)) + j // 2)

            pair(0, 0)
            with pool.Fori(0, (NP - 6) // 2) as i:
                pair(2 * i + 1, 1)
                pair(2 * i + 2, 0)
            for p in range(NP - 5, NP - 1):
                pair(p, p % 2)
            pair(NP - 1, 1, last=True)

            for g in range(2):
                pool.wait_ge(var_ready, g + 1)
                pool.tensor_tensor(rstd[:, 2 * g:2 * g + 2], vare[:, 2 * g:2 * g + 2], mhalf[:, 0:2], ALU.pow
                                   ).then_inc(rstd_ready, 1)
            mark_experts()
            for t in range(NT):
                pool.wait_ge(var_ready, 3 + t)
                pool.tensor_tensor(rstd[:, t:t + 1], vare[:, t:t + 1], mhalf[:, 0:1], ALU.pow).then_inc(rstd_ready, 1)
            pool.wait_ge(base_b_landed, 16)
            for t in range(NT):
                pool.wait_ge(x3_normed, t + 1)
                pool.tensor_tensor(x_res[:, t, :], x_res[:, t, :], bb_b[:], ALU.add).then_inc(base_b_added, 1)

        @block.vector
        def _(dve):
            links = 0

            def link(ins):
                nonlocal links
                links += 1
                ins.then_inc(chain, 1)
                dve.wait_ge(chain, links)

            def later(ins):
                nonlocal links
                links += 1
                ins.then_inc(chain, 1)
                return links

            def done(n):
                dve.wait_ge(chain, n)

            def x_stats(t):
                dve.wait_ge(x_landed[t], 16)
                return later(dve.bn_stats(stats[:, t, :], xin[:, t, :]))

            def aggregate(t, n):
                done(n)
                return later(dve.bn_aggr(mv[:, t, :], stats[:, t, :]))

            def x_variance(t, n):
                done(n)
                dve.tensor_scalar(vare[:, t:t + 1], mv[:, t, 1:2], EPS_LN, None, ALU.add).then_inc(ln_var, 1)

            def normalise_x(t):
                dve.wait_ge(ln_rstd, t + 1)
                dve.tensor_scalar(xin[:, t, :], xin[:, t, :], mv[:, t, 0:1], rstd[:, t:t + 1],
                                  ALU.subtract, ALU.mult).then_inc(ln_done, 1)

            st0 = x_stats(0)
            st1 = x_stats(1)
            ag0 = aggregate(0, st0)
            st2 = x_stats(2)
            x_variance(0, ag0)
            ag1 = aggregate(1, st1)
            st3 = x_stats(3)
            x_variance(1, ag1)
            ag2 = aggregate(2, st2)
            normalise_x(0)
            x_variance(2, ag2)
            ag3 = aggregate(3, st3)
            normalise_x(1)
            x_variance(3, ag3)
            normalise_x(2)
            normalise_x(3)

            def weights_lo(i, r, before):
                dve.wait_ge(w_hi_done, before + 4 * i + r + 1)
                n = r % 2
                dve.tensor_tensor(w_lo[:, n, 0:NC * DH], raw[:, r, :], w_hi[:, n, 0:NC * DH], ALU.subtract
                                  ).then_inc(w_lo_dve, 1)

            def norm_k(i, r):
                h = 4 * i + r
                dve.scalar_tensor_tensor(out=head(k_all, h), in0=head(k_all, h), scalar=column(g_c, h),
                                         in1=rkb[:], op0=ALU.mult, op1=ALU.mult).then_inc(k_normed, 1)

            weights_lo(0, 0, 0)
            for t in range(NT):
                dve.wait_ge(xt_hi, t + 1)
                tt = slice(t * P, (t + 1) * P)
                dve.tensor_tensor(xnt_lo[:, :, tt], p_flat[t].rearrange("p (c n) -> p c n", c=NC),
                                  xnt_hi[:, :, tt], ALU.subtract).then_inc(xt_lo, 1)
            for r in range(1, 4):
                weights_lo(0, r, 0)
            dve.wait_ge(const_landed, 16 * 5)
            link(dve.scalar_tensor_tensor(out=g_c[:], in0=g_c[:], scalar=float(DH) ** -0.5, in1=gq_c[:],
                                          op0=ALU.mult, op1=ALU.mult))
            with dve.Fori(1, NH // 4) as i:
                for r in range(4):
                    weights_lo(i, r, 0)

            def mean_squares(src, n):
                dve.wait_ge(ssq_ready, n)
                dve.tensor_scalar(ssq[:], src[:, 0:NT], 1.0 / INNER, EPS_RMS, ALU.mult, ALU.add
                                  ).then_inc(ssq_out, 1)

            for r in range(3):
                weights_lo(0, r, NH)
            mean_squares(p_flat[0], 1)
            dve.wait_ge(rms_done, 1)
            for t in range(NT):
                dve.tensor_scalar(diag[:, t, :], ident[:], rk_t[:, t:t + 1], None, ALU.mult).then_inc(diag_made, 1)
            weights_lo(0, 3, NH)
            dve.wait_ge(rkb_ready, 1)
            link(dve.tensor_copy(rkb[:], p_flat[1]))
            for r in range(4):
                weights_lo(1, r, NH)
                norm_k(0, r)
                norm_k(1, r)
            with dve.Fori(2, NH // 4) as i:
                for r in range(4):
                    weights_lo(i, r, NH)
                    norm_k(i, r)

            def slot_max(h, b):
                s = 2 * h + b
                dve.wait_ge(scores_ready, s + 1)
                dve.tensor_reduce(nmax[:, b, :], p_s[:], AX.X, ALU.max, negate=True).then_inc(max_done, 1)
                dve.wait_ge(max_done, s + 1)
                dve.tensor_tensor(nbias[:, b, :], nmax[:, b, :], rq_t[:, 2 * b:2 * b + 2], ALU.mult
                                  ).then_inc(nb_done, 1)

            def slot_norm(h, b):
                s = 2 * h + b
                dve.wait_ge(exp_done, 2 * s + 2)
                dve.reciprocal(rinv[:, b, :], rsum[:, b, :]).then_inc(rinv_done, 1)
                dve.wait_ge(rinv_done, s + 1)
                dve.tensor_scalar(probs[:, b, 0, :], probs[:, b, 0, :], rinv[:, b, 0:1], None, ALU.mult)
                dve.tensor_scalar(probs[:, b, 1, :], probs[:, b, 1, :], rinv[:, b, 1:2], None, ALU.mult
                                  ).then_inc(p_normed, 1)

            def v_half_lo(pair, e, par):
                dve.wait_ge(v_hi_done, 2 * pair + e + 1)
                dve.tensor_tensor(v_lo[:, par, 2 * e:2 * e + 2, :], p_v[:], v_hi[:, par, 2 * e:2 * e + 2, :],
                                  ALU.subtract).then_inc(v_lo_done, 1)

            def out_lo(h):
                dve.wait_ge(o_hi_done, h + 1)
                dve.scalar_tensor_tensor(out=o_lo[:], in0=p_o[:], scalar=column(bv_c, h), in1=o_hi[:],
                                         op0=ALU.add, op1=ALU.subtract).then_inc(o_lo_done, 1)

            def first_pairs_lo(n):
                dve.wait_ge(w_hi_done, U1 + n + 1)
                cols = slice(n % 2 * 512, n % 2 * 512 + 512)
                dve.tensor_tensor(w_lo[:, n // 2, cols], raw[:, n % 2, :], w_hi[:, n // 2, cols], ALU.subtract
                                  ).then_inc(w_lo_dve, 1)

            first_pairs_lo(0)
            first_pairs_lo(1)
            dve.wait_ge(kq_hi, 2)
            dve.tensor_tensor(k_lo[:], k_all[:, 0, :], k_hi[:], ALU.subtract).then_inc(kq_lo, 1)
            dve.tensor_tensor(q_lo[:], q_all[:, 0, :], q_hi[:], ALU.subtract).then_inc(kq_lo, 1)
            first_pairs_lo(2)
            v_half_lo(0, 0, 0)
            mean_squares(p_flat[2], 2)
            first_pairs_lo(3)
            dve.wait_ge(rms_done, 2)
            slot_max(0, 0)
            slot_norm(0, 0)
            v_half_lo(0, 1, 0)

            def last_out_lo(b):
                dve.wait_ge(o_hi_done, NH + b)
                cols = slice(b * S, (b + 1) * S)
                dve.scalar_tensor_tensor(out=o_last_lo[:, cols], in0=(p_o[:] if b == 0 else p_flat[0])[:, cols],
                                         scalar=bv_c[:, NH - 1:NH], in1=o_last_hi[:, cols], op0=ALU.add,
                                         op1=ALU.subtract).then_inc(o_lo_done, 1)

            def quantise_ctx(n, step):
                c = ctx_f[:, n, :]
                if step == 0:
                    dve.tensor_scalar(c, c, qc[:, 1:2], qs_b[:, 3:4], ALU.mult, ALU.add).then_inc(ctx_step, 1)
                elif step == 1:
                    dve.wait_ge(ctx_step, 2 * n + 1)
                    dve.tensor_scalar(c, c, QMIN, QMAX, ALU.max, ALU.min).then_inc(ctx_step, 1)
                else:
                    dve.wait_ge(ctx_step, 2 * n + 2)
                    dve.tensor_scalar(ctx_q[:, n, :], c, ROUND, ROUND + MID, ALU.add, ALU.subtract
                                      ).then_inc(ctx_quantised, 1)

            def pair(p, par, last=False, ctx_from=None):
                for j in range(4):
                    b = j % 2
                    h = 2 * p + j // 2
                    s = 2 * h + b
                    end = last and j == 3
                    if b == 0 and not peeled(h, 0, 1):
                        out_lo(h - 1)
                    if not end:
                        slot_max(h + b, 1 - b)
                    if end:
                        last_out_lo(0)
                    dve.wait_ge(pt_hi_done, s + 1)
                    dve.tensor_tensor(pt_lo[:], p_t[:], pt_hi[:], ALU.subtract).then_inc(pt_lo_done, 1)
                    if not end:
                        slot_norm(h + b, 1 - b)
                    if b == 1 and not last:
                        v_half_lo(p + 1, j // 2, 1 - par)
                    if ctx_from is not None:
                        for step in ((2,) if b else (0, 1)):
                            quantise_ctx(ctx_from + j // 2, step)

            pair(0, 0)
            with dve.Fori(0, (NP - 6) // 2) as i:
                pair(2 * i + 1, 1)
                pair(2 * i + 2, 0)
            dve.wait_ge(qs_landed, 16)
            dve.reciprocal(qc[:, 0:1], qs_b[:, 0:1])
            dve.reciprocal(qc[:, 1:2], qs_b[:, 2:3])
            dve.tensor_tensor(qc[:, 2:3], qs_b[:, 0:1], qs_b[:, 2:3], ALU.mult)
            dve.tensor_scalar(qc[:, 3:4], qs_b[:, 1:2], -1.0, MID, ALU.mult, ALU.add)
            link(dve.tensor_scalar(qc[:, 4:5], qs_b[:, 3:4], -1.0, MID, ALU.mult, ALU.add))
            link(dve.tensor_tensor(qc[:, 3:4], qc[:, 3:4], qc[:, 2:3], ALU.mult))
            dve.tensor_tensor(qc[:, 5:6], qc[:, 4:5], qc[:, 2:3], ALU.mult)
            link(dve.scalar_tensor_tensor(out=qc[:, 6:7], in0=qc[:, 4:5], scalar=float(D), in1=qc[:, 3:4],
                                          op0=ALU.mult, op1=ALU.mult))
            dve.wait_ge(ctx_landed, 32)
            for p in range(NP - 5, NP - 1):
                pair(p, p % 2, ctx_from=2 * (p - (NP - 5)))
            pair(NP - 1, 1, last=True)

            def pair_stats(g):
                for t in (2 * g, 2 * g + 1):
                    dve.wait_ge(x1_ready, t + 1)
                    n = later(dve.bn_stats(stats[:, t, :], acc[t][:]))
                return n

            def pair_variance(g, n):
                t0 = 2 * g
                done(n)
                later(dve.bn_aggr(mv[:, t0, :], stats[:, t0, :]))
                done(later(dve.bn_aggr(mv[:, t0 + 1, :], stats[:, t0 + 1, :])))
                dve.tensor_scalar(vare[:, t0:t0 + 2], mv[:, t0:t0 + 2, 1], EPS_LN, None, ALU.add
                                  ).then_inc(var_ready, 1)

            def pair_coefficients(g):
                a = slice(2 * g, 2 * g + 2)
                dve.wait_ge(rstd_ready, g + 1)
                link(dve.tensor_scalar(cs[:, a], rstd[:, a], qc[:, 0:1], None, ALU.mult))
                link(dve.tensor_tensor(cm[:, a], mv[:, a, 0], cs[:, a], ALU.mult))
                dve.tensor_scalar(cb[:, a], cm[:, a], -1.0, qs_b[:, 1:2], ALU.mult, ALU.add).then_inc(coef_ready, 1)

            def quantise(t0):
                n = [0, 0]
                for k in range(2):
                    t = t0 + k
                    dve.wait_ge(linear_done, t + 1)
                    n[k] = later(dve.tensor_scalar(xn[:, t, :], xn[:, t, :], QMIN, QMAX, ALU.max, ALU.min))
                    if k == 1:
                        done(n[0])
                        dve.tensor_scalar(q1[:, t0, :], xn[:, t0, :], ROUND, ROUND + MID, ALU.add, ALU.subtract
                                          ).then_inc(q1_done, 1)
                done(n[1])
                dve.tensor_scalar(q1[:, t0 + 1, :], xn[:, t0 + 1, :], ROUND, ROUND + MID, ALU.add, ALU.subtract
                                  ).then_inc(q1_done, 1)

            def second_sum(t):
                dve.wait_ge(scaled_done, t + 1)
                dve.tensor_tensor(x_res[:, t, :], acc[t][:], xn[:, t, :], ALU.add).then_inc(x2_done, 1)

            def stats3(t):
                dve.wait_ge(x2_done, t + 1)
                return later(dve.bn_stats(stats[:, t, :], x_res[:, t, :]))

            def variance3(t, n):
                done(n)
                link(dve.bn_aggr(mv[:, t, :], stats[:, t, :]))
                dve.tensor_scalar(vare[:, t:t + 1], mv[:, t, 1:2], EPS_LN, None, ALU.add).then_inc(var_ready, 1)

            def bias3(t):
                dve.wait_ge(rstd_ready, 3 + t)
                dve.scalar_tensor_tensor(out=cb[:, t:t + 1], in0=mv[:, t, 0:1], scalar=-1.0,
                                         in1=rstd[:, t:t + 1], op0=ALU.mult, op1=ALU.mult).then_inc(coef_ready, 1)

            def x3_lo(t):
                dve.wait_ge(x3_hi_done, t + 1)
                tt = slice(t * P, (t + 1) * P)
                dve.tensor_tensor(xnt_lo[:, :, tt], acc[t][:].rearrange("p (c n) -> p c n", c=NC),
                                  xnt_hi[:, :, tt], ALU.subtract).then_inc(x3_lo_done, 1)

            n = pair_stats(0)
            last_out_lo(1)
            pair_variance(0, n)
            pair_coefficients(0)
            n = pair_stats(1)
            pair_variance(1, n)
            quantise(0)
            pair_coefficients(1)
            quantise(2)
            second_sum(0)
            n0 = stats3(0)
            second_sum(1)
            variance3(0, n0)
            n1 = stats3(1)
            bias3(0)
            variance3(1, n1)
            bias3(1)
            second_sum(2)
            x3_lo(0)
            n2 = stats3(2)
            x3_lo(1)
            variance3(2, n2)
            second_sum(3)
            n3 = stats3(3)
            bias3(2)
            variance3(3, n3)
            bias3(3)
            x3_lo(2)
            x3_lo(3)
            dve.wait_ge(router_b_landed, 16)
            for t in range(NT):
                dve.wait_ge(low_rank_ready, t + 1)
                n = later(dve.tensor_tensor(logit[:, t, :], acc[t][:, P:P + NR], rb_b[:], ALU.add))
            done(n)

            def wide(a):
                return a.unsqueeze(2).to_broadcast([P, NT, NR])

            link(dve.tensor_reduce(fsm[:, 0:NT], logit[:], AX.X, ALU.max))
            dve.tensor_tensor(logit[:], logit[:], wide(fsm[:, 0:NT]), ALU.subtract).then_inc(max_taken, 1)
            dve.wait_ge(router_exp_done, 1)
            link(dve.tensor_reduce(fsm[:, NT:2 * NT], pr[:], AX.X, ALU.add))
            link(dve.reciprocal(fsm[:, 2 * NT:3 * NT], fsm[:, NT:2 * NT]))
            link(dve.tensor_tensor(pr[:], pr[:], wide(fsm[:, 2 * NT:3 * NT]), ALU.mult))
            for t in range(NT):
                n = later(dve.max(out=top8[:, t, :], in_=pr[:, t, :]))
            done(n)
            for t in range(NT):
                n = later(dve.match_replace(out=cut[:, t, :], in_to_replace=top8[:, t, :], in_values=pr[:, t, :],
                                            imm_value=-1.0))
            done(n)
            link(dve.scalar_tensor_tensor(out=kept[:], in0=cut[:], scalar=0.0, in1=pr[:],
                                          op0=ALU.is_lt, op1=ALU.mult))
            dve.wait_ge(experts_marked, 1)
            for t in range(NT):
                n = later(dve.tensor_tensor(spread[:, t, :, :], kept[:, t, :].unsqueeze(1).to_broadcast([P, NE, NR]),
                                            onehot[:], ALU.mult))
            done(n)
            link(dve.tensor_reduce(gate[:], spread[:], AX.X, ALU.add))
            for t in range(NT):
                ins = dve.scalar_tensor_tensor(out=hw[:, t, :].rearrange("p (e r) -> p e r", e=NE),
                                               in0=acc[t][:, 0:P].rearrange("p (e r) -> p e r", e=NE), scalar=2.0,
                                               in1=gate[:, t, :].unsqueeze(2).to_broadcast([P, NE, RK]),
                                               op0=ALU.mult, op1=ALU.mult)
            ins.then_inc(hw_done, 1)
            dve.wait_ge(hwt_hi_done, 1)
            dve.tensor_tensor(hwt_lo[:].rearrange("p t n -> p (t n)"), acc[0][:],
                              hwt_hi[:].rearrange("p t n -> p (t n)"), ALU.subtract).then_inc(hwt_lo_done, 1)
            for t in range(NT):
                dve.wait_ge(base_b_added, t + 1)
                dve.wait_ge(y_ready, t + 1)
                dve.tensor_tensor(xn[:, t, :], p_flat[t], x_res[:, t, :], ALU.add).then_inc(out_done, 1)


def kernel(**inputs):
    import numpy as np
    from concourse import bacc
    from concourse.bass_utils import run_bass_kernel_spmd

    a = {k: np.asarray(v) for k, v in inputs.items()}

    def per_head(w):
        return np.ascontiguousarray(w.reshape(NC, P, NH, DH).transpose(2, 1, 0, 3)).reshape(NH, P, NC * DH)

    def per_pair(w):
        n = w.shape[1] // PW
        t = w.reshape(2, 2, P, n, PW).transpose(3, 0, 2, 1, 4)
        return np.ascontiguousarray(t).reshape(2 * n, P, 2 * PW)

    def columns(v):
        return np.ascontiguousarray(v.reshape(NH, DH).T)

    wv_base = np.concatenate([a["L0_attn_Wv"], a["L0_ffn_base_W"].T], axis=1)
    a_r = np.concatenate([a["L0_ffn_A"].reshape(NE * RK, D), a["L0_ffn_router_W"],
                          np.zeros((1, D), np.float32)], axis=0)
    arrays = {
        "in_x": a["x"].reshape(NT, P, D),
        "in_ctx": np.ascontiguousarray(a["ctx_4096"].reshape(B * NC, P, SKV).transpose(1, 0, 2)),
        "in_wk": per_head(a["L0_attn_Wk"]),
        "in_wq": per_head(a["L0_attn_Wq"]),
        "in_wv": per_pair(wv_base),
        "in_wo": a["L0_attn_Wo"].reshape(NH, DH, D),
        "in_bk": columns(a["L0_attn_bk"]),
        "in_bq": columns(a["L0_attn_bq"]),
        "in_bv": columns(a["L0_attn_bv"]),
        "in_bo": a["L0_attn_bo"],
        "in_gk": columns(a["L0_attn_gk"]),
        "in_gq": columns(a["L0_attn_gq"]),
        "in_qs": np.concatenate([a["L0_xattn_x1_scale"], a["L0_xattn_x1_zp"], a["L0_xattn_x2_scale"],
                                 a["L0_xattn_x2_zp"]]),
        "in_ra": np.ascontiguousarray(a_r.T.reshape(NC, P, RA).transpose(1, 0, 2)).reshape(P, NC * RA),
        "in_bb": a["L0_ffn_base_b"],
        "in_rb": a["L0_ffn_router_b"],
        "in_bm": np.ascontiguousarray(a["L0_ffn_B"].transpose(0, 2, 1)).reshape(NE * RK, D),
        "in_em": a["L0_ffn_expert_map"],
    }
    nc = bacc.Bacc("TRN2", target_bir_lowering=False, num_devices=1)
    args = [nc.dram_tensor(k, v.shape, mybir.dt.from_np(v.dtype), kind="ExternalInput").ap()
            for k, v in arrays.items()]
    y = nc.dram_tensor("out_y", (NT, P, D), F32, kind="ExternalOutput").ap()
    decoder_layer(nc, *args, y)
    r = run_bass_kernel_spmd(nc, [arrays], core_ids=[0])
    return r.results[0]["out_y"].reshape(B, S, D)
```
